# Optimizing a Trainium2 kernel written in Bass

```python
import numpy as np
import jax
import jax.numpy as jnp

def _softmax(x, axis=-1):
    return jax.nn.softmax(x, axis=axis)

def _gelu(x):
    return jax.nn.gelu(x, approximate=True)

def _silu(x):
    return jax.nn.silu(x)

def _sigmoid(x):
    return jax.nn.sigmoid(x)

def _layernorm(x, axis=-1, eps=1e-05):
    m = jnp.mean(x, axis=axis, keepdims=True)
    v = jnp.var(x, axis=axis, keepdims=True)
    return (x - m) / jnp.sqrt(v + eps)

def _scatter_add(tgt, idx, src, axis=0):
    return tgt.at[idx].add(src)

def _segment_sum(src, seg, n):
    return jax.ops.segment_sum(src, seg, n)
kernel_name = 'mk_gnn_resnorm_d1_gnn_r8_f7e9a5'

def setup_inputs(seed: int=0):
    np.random.seed(seed)
    _w = jnp.asarray

    def _rec_inputs():
        import jax
        import jax.numpy as jnp
        _gk = jax.random.key(seed)
        x = -0.000202 + 1 * jax.random.normal(jax.random.fold_in(_gk, 1), (12500, 64), jnp.float32)
        src = jax.random.randint(jax.random.fold_in(_gk, 2), (400000,), 0, 12500, jnp.int32)
        dst = jax.random.randint(jax.random.fold_in(_gk, 3), (400000,), 0, 12500, jnp.int32)
        _o = jnp.argsort(dst, stable=True)
        src = src[_o]
        dst = dst[_o]
        edge_attr_64 = -8.16379e-05 + 0.999858 * jax.random.normal(jax.random.fold_in(_gk, 12), (400000, 64), jnp.float32)
        edge_weight1 = jax.random.uniform(jax.random.fold_in(_gk, 13), (400000, 1), jnp.float32, 0.0, 0.999999)
        return (x, src, dst, edge_attr_64, edge_weight1)
    x, src, dst, edge_attr_64, edge_weight1 = _rec_inputs()

    def _L0_gnn_setup():
        import jax, jax.numpy as jnp
        import numpy as np
        N_SRC = 12500
        N_DST = 12500
        N_EDGES = 200000
        HID = 64
        key = jax.random.key(seed)
        ks = jax.random.split(key, 7)
        feat_src = jax.random.normal(ks[0], (N_SRC, HID), dtype=jnp.float32)
        review_feat = jax.random.normal(ks[1], (N_EDGES, HID), dtype=jnp.float32)
        edge_w = jax.random.uniform(ks[2], (N_EDGES, 1), dtype=jnp.float32)
        bound = float(np.sqrt(6.0 / (HID + HID)))
        node_w = jax.random.uniform(ks[3], (HID, HID), dtype=jnp.float32, minval=-bound, maxval=bound)
        review_w = jax.random.uniform(ks[4], (HID, HID), dtype=jnp.float32, minval=-bound, maxval=bound)
        src_idx = jax.random.randint(ks[5], (N_EDGES,), 0, N_SRC, dtype=jnp.int32)
        dst_idx = jax.random.randint(ks[6], (N_EDGES,), 0, N_DST, dtype=jnp.int32)
        return {'feat_src': feat_src, 'review_feat': review_feat, 'edge_w': edge_w, 'node_w': node_w, 'review_w': review_w, 'src_idx': src_idx, 'dst_idx': dst_idx}
    _L0_gnn_all = _L0_gnn_setup()
    _L0_gnn_in = {k: v for k, v in _L0_gnn_all.items() if k in ('node_w', 'review_w')}
    del _L0_gnn_all
    return {'x': x, 'src': src, 'dst': dst, 'edge_attr_64': edge_attr_64, 'edge_weight1': edge_weight1, 'L0_gnn_node_w': _L0_gnn_in['node_w'], 'L0_gnn_review_w': _L0_gnn_in['review_w']}

def reference(x, src, dst, edge_attr_64, edge_weight1, L0_gnn_node_w, L0_gnn_review_w):
    import jax
    import jax.numpy as jnp

    def _L0_gnn_ref(feat_src, review_feat, edge_w, node_w, review_w, src_idx, dst_idx):
        import jax, jax.numpy as jnp
        import numpy as np
        N_SRC = 12500
        N_DST = 12500
        N_EDGES = 200000
        HID = 64
        h = feat_src @ node_w.T
        rf = review_feat @ review_w.T
        m = (h[src_idx] + rf) * edge_w
        return jax.ops.segment_sum(m, dst_idx, num_segments=N_DST)
    x = _layernorm(x + _L0_gnn_ref(x, edge_attr_64, edge_weight1, L0_gnn_node_w, L0_gnn_review_w, src, dst), axis=-1)
    return x

_drawn_inputs = setup_inputs


def setup_inputs(seed=0):
    import zlib

    import numpy as np

    out = dict(_drawn_inputs(seed))
    spreads = {}
    factors = {}
    for name, (base, spread) in spreads.items():
        noise = np.random.default_rng([zlib.crc32(name.encode()), seed]).standard_normal(out[name].shape)
        drawn = base * np.exp(spread * noise) if base else spread * noise
        out[name] = jnp.asarray(drawn.astype(out[name].dtype))
    for name, factor in factors.items():
        out[name] = (out[name] * factor).astype(out[name].dtype)
    return out
```

```python
from contextlib import ExitStack

import concourse.bass as bass
from concourse import mybir

ALU = mybir.AluOpType
ACT = mybir.ActivationFunctionType
F32 = mybir.dt.float32
I32 = mybir.dt.int32
U32 = mybir.dt.uint32
AX_X = mybir.AxisListType.X

P = 128
TILES = 25
SLOTS = 5
PARTS = 5
WIN = 128
WIN_SHIFT = 7
LN_EPS = 1e-5


def build(nc, x, src, dst, attr, weight, node_w, review_w, out):
    NODES, F = x.shape
    EDGES = src.shape[0]
    CHUNK = P * TILES
    CHUNKS = EDGES // CHUNK
    ROUNDS = CHUNKS // SLOTS
    PER_PART = TILES // PARTS
    assert EDGES == CHUNKS * CHUNK and CHUNKS == ROUNDS * SLOTS and CHUNKS <= P and 2 * F == P
    assert TILES == PARTS * PER_PART and WIN == 1 << WIN_SHIFT
    MAX_WINDOWS = (NODES - 1) // WIN + 1
    ALL_WINDOWS = MAX_WINDOWS * CHUNKS

    J = 8
    groups = [(g * P * J, P, J) for g in range(NODES // (P * J))]
    rest = NODES - len(groups) * P * J
    if rest:
        j = next(j for j in range(1, J + 1) if rest % j == 0 and rest // j <= P)
        groups.append((NODES - rest, rest // j, j))
    GROUPS = len(groups)

    with ExitStack() as ctx:
        def sb(name, shape, dt=F32):
            return ctx.enter_context(nc.sbuf_tensor(name, shape, dt))

        def ps(name, shape, dt=F32):
            return ctx.enter_context(nc.psum_tensor(name, shape, dt))

        def sem(name):
            return ctx.enter_context(nc.semaphore(name))

        sums = sb("sums", [P, NODES + WIN])
        dst_i = sb("dst_i", [P, CHUNKS, TILES], I32)
        dst_f = dst_i[:, :, :].bitcast(F32)
        rows = [sb(f"rows{s}", [P, TILES, 2 * F]) for s in range(SLOTS)]
        src_sb = [sb(f"src{s}", [P, TILES], I32) for s in range(SLOTS)]
        w_sb = [sb(f"w{s}", [P, TILES]) for s in range(SLOTS)]
        dst_left = sb("dst_left", [P, TILES])
        scatter = sb("scatter", [P, TILES, WIN])
        column = sb("column", [P, WIN])
        column_i = sb("column_i", [P, WIN], I32)
        ident = sb("ident", [P, P])
        ones = sb("ones", [P, P])
        lo_hi = sb("lo_hi", [P, 2, CHUNKS])
        lo_hi_col = sb("lo_hi_col", [CHUNKS, 2])
        lo_diag = sb("lo_diag", [CHUNKS, CHUNKS])
        lo_hi_row = sb("lo_hi_row", [1, 2, CHUNKS])
        lo_all = sb("lo_all", [P, CHUNKS])
        span_i = sb("span_i", [1, CHUNKS], I32)
        windows_i = sb("windows_i", [1, CHUNKS], I32)
        windows_f = sb("windows_f", [1, CHUNKS])
        until_f = sb("until_f", [1, CHUNKS])
        base_tab = sb("base_tab", [1, CHUNKS], I32)
        window_tab = sb("window_tab", [1, CHUNKS + 1], I32)
        w_both = sb("w_both", [F, 2 * F])
        w_t = sb("w_t", [2 * F, F])
        nodes = sb("nodes", [P, GROUPS, J, F])
        square = sb("square", [P, 2, J, F])
        mean = sb("mean", [P, GROUPS, J])
        var = sb("var", [P, GROUPS, J])
        std = sb("std", [P, GROUPS, J])
        rstd = sb("rstd", [P, GROUPS, J])
        eps = sb("eps", [P, 1])

        window_ps = ps("window_ps", [P, 512])
        table_ps = ps("table_ps", [P, 512])
        row_ps = ps("row_ps", [P, 512])
        out_ps = [ps(f"out_ps{b}", [P, J, F]) for b in range(2)]

        dst_loaded = sem("dst_loaded")
        w_loaded = sem("w_loaded")
        nodes_loaded = sem("nodes_loaded")
        pool_made = sem("pool_made")
        consts_ready = sem("consts_ready")
        dve_step = sem("dve_step")
        lo_hi_ready = sem("lo_hi_ready")
        lo_hi_turned = sem("lo_hi_turned")
        col_ready = sem("col_ready")
        diag_ready = sem("diag_ready")
        rows_turned = sem("rows_turned")
        tables_ready = sem("tables_ready")
        w_turned = sem("w_turned")
        w_t_ready = sem("w_t_ready")
        src_landed = [sem(f"src_landed{s}") for s in range(SLOTS)]
        edge_landed = [sem(f"edge_landed{s}") for s in range(SLOTS)]
        gathers_begun = sem("gathers_begun")
        gathered = [sem(f"gathered{s}") for s in range(SLOTS)]
        slot_free = [sem(f"slot_free{s}") for s in range(SLOTS)]
        scatter_ready = [sem(f"scatter_ready{q}") for q in range(PARTS)]
        window_summed = sem("window_summed")
        window_added = sem("window_added")
        left_ready = sem("left_ready")
        sums_ready = sem("sums_ready")
        out_multiplied = sem("out_multiplied")
        out_added = sem("out_added")
        mean_ready = sem("mean_ready")
        centred = sem("centred")
        squared = sem("squared")
        var_ready = sem("var_ready")
        std_ready = sem("std_ready")
        rstd_ready = sem("rstd_ready")
        scaled = sem("scaled")
        stored = sem("stored")

        block = ctx.enter_context(nc.Block())

        def by_partition(dram, c):
            return dram[bass.ds(c * CHUNK, CHUNK)].rearrange("(p k) -> p k", k=TILES)

        @block.sync
        def _(sp):
            sp.dma_start(dst_i[:, :, :], dst.rearrange("(c p k) -> p c k", p=P, k=TILES)).then_inc(dst_loaded, 16)
            sp.dma_start(w_both[:, 0:F], node_w).then_inc(w_loaded, 16)
            sp.dma_start(w_both[:, F:2 * F], review_w).then_inc(w_loaded, 16)
            with sp.Fori(0, ROUNDS) as r:
                for s in range(SLOTS):
                    c = r * SLOTS + s
                    sp.wait_ge(slot_free[s], r + 1)
                    sp.dma_start(src_sb[s][:, :], by_partition(src, c)).then_inc(src_landed[s], 16)
                    sp.dma_start(w_sb[s][:, :], by_partition(weight.rearrange("e a -> (e a)"), c)).then_inc(edge_landed[s], 16)
                    sp.dma_start(rows[s][:, :, F:2 * F],
                                 attr[bass.ds(c * CHUNK, CHUNK), :].rearrange("(p k) f -> p k f", k=TILES)
                                 ).then_inc(edge_landed[s], 16)
            for g, (n0, np_, j) in enumerate(groups):
                sp.dma_start(nodes[0:np_, g, 0:j, :],
                             x[n0:n0 + np_ * j, :].rearrange("(p j) f -> p j f", j=j)).then_inc(nodes_loaded, 16)
            for g, (n0, np_, j) in enumerate(groups):
                sp.wait_ge(scaled, g + 1)
                sp.dma_start(out[n0:n0 + np_ * j, :].rearrange("(p j) f -> p j f", j=j),
                             nodes[0:np_, g, 0:j, :]).then_inc(stored, 16)
            sp.wait_ge(stored, 16 * GROUPS)

        @block.gpsimd
        def _(pool):
            def scale_rows(g):
                n0, np_, j = groups[g]
                y = nodes[0:np_, g, 0:j, :]
                pool.wait_ge(rstd_ready, g + 1)
                pool.wait_ge(squared, g + 1)
                pool.wait_ge(centred, g + 1)
                pool.tensor_tensor(y, y, rstd[0:np_, g, 0:j].unsqueeze(2).to_broadcast([np_, j, F]), ALU.mult
                                   ).then_inc(scaled, 1)

            pool.memset(ident[:, :], 0.0).then_inc(pool_made, 1)
            pool.iota(column_i[:, :], pattern=[[1, WIN]], base=0, channel_multiplier=0).then_inc(pool_made, 1)
            pool.wait_ge(pool_made, 2)
            pool.affine_select(out=ident[:, :], in_=ident[:, :], compare_op=ALU.not_equal, fill=1.0,
                               base=0, pattern=[[-1, P]], channel_multiplier=1).then_inc(pool_made, 1)
            with pool.Fori(0, ROUNDS) as r:
                for s in range(SLOTS):
                    pool.wait_ge(src_landed[s], (r + 1) * 16)
                    pool.wait_ge(slot_free[s], r + 1)
                    pool.sem_inc(gathers_begun, 1)
                    for k in range(TILES):
                        pool.indirect_dma_start(
                            out=rows[s][:, k, 0:F], out_offset=None, in_=x,
                            in_offset=bass.IndirectOffsetOnAxis(ap=src_sb[s][:, k:k + 1].bitcast(U32), axis=0),
                        ).then_inc(gathered[s], 16)
            for g, (n0, np_, j) in enumerate(groups):
                y = nodes[0:np_, g, 0:j, :]
                pool.wait_ge(mean_ready, g + 1)
                pool.tensor_tensor(y, y, mean[0:np_, g, 0:j].unsqueeze(2).to_broadcast([np_, j, F]), ALU.subtract
                                   ).then_inc(centred, 1)
                if g >= 1:
                    scale_rows(g - 1)
            scale_rows(GROUPS - 1)

        @block.vector
        def _(dve):
            steps = 0

            def step(ins):
                nonlocal steps
                steps += 1
                ins.then_inc(dve_step, 1)
                dve.wait_ge(dve_step, steps)

            for s in range(SLOTS):
                dve.sem_inc(slot_free[s], 1)
            dve.memset(ones[:, :], 1.0)
            dve.memset(eps[:, :], LN_EPS)
            dve.wait_ge(pool_made, 3)
            dve.tensor_copy(column[:, :], column_i[:, :]).then_inc(consts_ready, 1)
            dve.wait_ge(dst_loaded, 16)
            step(dve.tensor_copy(dst_f, dst_i[:, :, :]))
            dve.tensor_reduce(lo_hi[:, 0, :], dst_f, AX_X, ALU.min)
            dve.tensor_reduce(lo_hi[:, 1, :], dst_f, AX_X, ALU.max).then_inc(lo_hi_ready, 1)
            dve.wait_ge(lo_hi_turned, 1)
            dve.tensor_reduce(lo_hi_col[:, 0:1], table_ps[0:CHUNKS, 0:P], AX_X, ALU.min)
            dve.tensor_reduce(lo_hi_col[:, 1:2], table_ps[0:CHUNKS, P:2 * P], AX_X, ALU.max).then_inc(col_ready, 1)
            dve.wait_ge(col_ready, 1)
            dve.tensor_scalar(lo_diag[:, :], ident[0:CHUNKS, 0:CHUNKS], lo_hi_col[:, 0:1], None, ALU.mult
                              ).then_inc(diag_ready, 1)
            dve.wait_ge(rows_turned, 1)
            dve.tensor_copy(lo_hi_row[0:1, :, :], row_ps[0:1, 0:2 * CHUNKS].rearrange("p (a c) -> p a c", a=2))
            step(dve.tensor_copy(lo_all[:, :], table_ps[:, 2 * P:2 * P + CHUNKS]))
            dve.tensor_tensor(dst_f, dst_f, lo_all[:, :].unsqueeze(2).to_broadcast([P, CHUNKS, TILES]), ALU.subtract)
            dve.tensor_copy(base_tab[0:1, :], lo_hi_row[0:1, 0, :])
            step(dve.tensor_tensor(span_i[:, :], lo_hi_row[0:1, 1, :], lo_hi_row[0:1, 0, :], ALU.subtract))
            step(dve.tensor_scalar(windows_i[:, :], span_i[:, :], WIN_SHIFT, None, ALU.arith_shift_right))
            step(dve.tensor_scalar(windows_f[:, :], windows_i[:, :], 1.0, None, ALU.add))
            step(dve.tensor_tensor_scan(until_f[:, :], ones[0:1, 0:CHUNKS], windows_f[:, :], 0.0, ALU.mult, ALU.add))
            dve.memset(window_tab[:, 0:1], 0)
            dve.tensor_copy(window_tab[:, 1:CHUNKS + 1], until_f[:, :]).then_inc(tables_ready, 1)
            dve.memset(sums[:, :], 0.0).then_inc(window_added, 1)
            dve.wait_ge(w_turned, 1)
            dve.tensor_copy(w_t[:, :], out_ps[1][:, 0, :]).then_inc(w_t_ready, 1)
            dve.wait_ge(tables_ready, 1)
            dve.sem_inc(left_ready, 1)

            with dve.Fori(0, ROUNDS) as r:
                for s in range(SLOTS):
                    c = r * SLOTS + s
                    base = dve.value_load(base_tab[0:1, bass.ds(c, 1)], min_val=0, max_val=NODES - 1)
                    first = dve.value_load(window_tab[0:1, bass.ds(c, 1)], min_val=0, max_val=ALL_WINDOWS)
                    until = dve.value_load(window_tab[0:1, bass.ds(c + 1, 1)], min_val=0, max_val=ALL_WINDOWS)
                    dve.wait_ge(edge_landed[s], (r + 1) * 32)
                    dve.wait_ge(left_ready, first + c + 1)
                    dve.tensor_copy(dst_left[:, :], dst_f[:, bass.ds(c, 1), :].rearrange("p a k -> p (a k)")
                                    ).then_inc(left_ready, 1)
                    with dve.Fori(first, until) as w:
                        dve.wait_ge(left_ready, w + c + 2)
                        for q in range(PARTS):
                            for k in range(q * PER_PART, (q + 1) * PER_PART):
                                made = dve.tensor_scalar(scatter[:, k, :], column[:, :], dst_left[:, k:k + 1],
                                                         w_sb[s][:, k:k + 1], ALU.is_equal, ALU.mult)
                            made.then_inc(scatter_ready[q], 1)
                        dve.wait_ge(window_summed, w + 1)
                        dve.wait_ge(window_added, w + 1)
                        dve.tensor_scalar(dst_left[:, :], dst_left[:, :], float(WIN), None, ALU.subtract
                                          ).then_inc(left_ready, 1)
                        at = nc.s_assert_within(
                            base + (w - first) * WIN, 0, NODES - 1, skip_runtime_bounds_check_because=
                            "a chunk's last window begins at or before its largest dst, which is a node")
                        dve.tensor_tensor(sums[:, bass.ds(at, WIN)], sums[:, bass.ds(at, WIN)],
                                          window_ps[:, 0:WIN], ALU.add).then_inc(window_added, 1)
                    dve.sem_inc(slot_free[s], 1)
            total = dve.value_load(window_tab[0:1, CHUNKS:CHUNKS + 1], min_val=0, max_val=ALL_WINDOWS)
            dve.wait_ge(window_added, total + 1)
            dve.sem_inc(sums_ready, 1)

            dve.wait_ge(nodes_loaded, 16 * GROUPS)
            for g in range(GROUPS + 1):
                if g < GROUPS:
                    n0, np_, j = groups[g]
                    y = nodes[0:np_, g, 0:j, :]
                    dve.wait_ge(out_multiplied, g + 1)
                    dve.tensor_tensor(y, y, out_ps[g % 2][0:np_, 0:j, :], ALU.add).then_inc(out_added, 1)
                    dve.wait_ge(out_added, g + 1)
                    step(dve.tensor_reduce(mean[0:np_, g, 0:j], y, AX_X, ALU.add))
                    dve.tensor_scalar(mean[0:np_, g, 0:j], mean[0:np_, g, 0:j], 1.0 / F, None, ALU.mult
                                      ).then_inc(mean_ready, 1)
                if g >= 1:
                    n0, np_, j = groups[g - 1]
                    dve.wait_ge(squared, g)
                    dve.tensor_reduce(var[0:np_, g - 1, 0:j], square[0:np_, (g - 1) % 2, 0:j, :], AX_X, ALU.add
                                      ).then_inc(var_ready, 1)
                    dve.wait_ge(std_ready, g)
                    dve.reciprocal(rstd[0:np_, g - 1, 0:j], std[0:np_, g - 1, 0:j]).then_inc(rstd_ready, 1)

        @block.scalar
        def _(act):
            act.wait_ge(consts_ready, 1)
            for g in range(GROUPS):
                n0, np_, j = groups[g]
                act.wait_ge(centred, g + 1)
                if g >= 2:
                    act.wait_ge(var_ready, g - 1)
                act.activation(square[0:np_, g % 2, 0:j, :], nodes[0:np_, g, 0:j, :], ACT.Square).then_inc(squared, 1)
                act.wait_ge(var_ready, g + 1)
                act.activation(std[0:np_, g, 0:j], var[0:np_, g, 0:j], ACT.Sqrt, bias=eps[0:np_, :], scale=1.0 / F
                               ).then_inc(std_ready, 1)

        @block.tensor
        def _(pe):
            pe.wait_ge(pool_made, 3)
            pe.wait_ge(lo_hi_ready, 1)
            pe.transpose(table_ps[0:CHUNKS, 0:P], lo_hi[:, 0, :], ident[:, :])
            pe.transpose(table_ps[0:CHUNKS, P:2 * P], lo_hi[:, 1, :], ident[:, :]).then_inc(lo_hi_turned, 1)
            pe.wait_ge(col_ready, 1)
            for a in range(2):
                pe.matmul(row_ps[0:1, a * CHUNKS:(a + 1) * CHUNKS], lo_hi_col[:, a:a + 1],
                          ident[0:CHUNKS, 0:CHUNKS], start=True, stop=True)
            pe.wait_ge(diag_ready, 1)
            pe.matmul(table_ps[:, 2 * P:2 * P + CHUNKS], ones[0:CHUNKS, :], lo_diag[:, :],
                      start=True, stop=True).then_inc(rows_turned, 1)
            pe.wait_ge(w_loaded, 32)
            pe.transpose(out_ps[1][:, 0, :], w_both[:, :], ident[0:F, 0:F]).then_inc(w_turned, 1)
            pe.wait_ge(tables_ready, 1)

            with pe.Fori(0, ROUNDS) as r:
                for s in range(SLOTS):
                    c = r * SLOTS + s
                    first = pe.value_load(window_tab[0:1, bass.ds(c, 1)], min_val=0, max_val=ALL_WINDOWS)
                    until = pe.value_load(window_tab[0:1, bass.ds(c + 1, 1)], min_val=0, max_val=ALL_WINDOWS)
                    with pe.Fori(first, until) as w:
                        pe.wait_ge(edge_landed[s], (r + 1) * 32)
                        pe.wait_ge(gathered[s], (r + 1) * (16 * TILES))
                        pe.wait_ge(window_added, w + 1)
                        for k in range(TILES):
                            if k % PER_PART == 0:
                                pe.wait_ge(scatter_ready[k // PER_PART], w + 1)
                            done = pe.matmul(window_ps[:, 0:WIN], rows[s][:, k, :], scatter[:, k, :],
                                             start=(k == 0), stop=(k == TILES - 1))
                        done.then_inc(window_summed, 1)

            pe.wait_ge(sums_ready, 1)
            pe.wait_ge(w_t_ready, 1)
            for g, (n0, np_, j) in enumerate(groups):
                if g >= 2:
                    pe.wait_ge(out_added, g - 1)
                for i in range(j):
                    last = pe.matmul(out_ps[g % 2][0:np_, i, :], sums[:, n0 + i:n0 + (np_ - 1) * j + i + 1:j],
                                     w_t[:, :], start=True, stop=True)
                last.then_inc(out_multiplied, 1)


INPUTS = ["x", "src", "dst", "edge_attr_64", "edge_weight1", "L0_gnn_node_w", "L0_gnn_review_w"]


def kernel(**inputs):
    import numpy as np
    import concourse.bacc as bacc
    from concourse.bass_utils import run_bass_kernel_spmd

    nc = bacc.Bacc("TRN2", target_bir_lowering=False, num_devices=1)
    arrays, args = {}, []
    for name in INPUTS:
        a = np.ascontiguousarray(inputs[name])
        arrays[name] = a
        args.append(nc.dram_tensor(name, a.shape, mybir.dt.from_np(a.dtype), kind="ExternalInput").ap())
    out = nc.dram_tensor("out", arrays["x"].shape, F32, kind="ExternalOutput").ap()
    build(nc, *args, out)
    result = run_bass_kernel_spmd(nc, [arrays], core_ids=[0])
    return result.results[0]["out"]
```

```python
from contextlib import ExitStack

import concourse.bass as bass
from concourse import mybir

ALU = mybir.AluOpType
ACT = mybir.ActivationFunctionType
F32 = mybir.dt.float32
F16 = mybir.dt.float16
BF16 = mybir.dt.bfloat16
I32 = mybir.dt.int32
U32 = mybir.dt.uint32
AX_X = mybir.AxisListType.X

P = 128
LO_BITS = 7
TILES = 25
SLOTS = 4
PARTS = 5
WIN = 128
WIN_SHIFT = 7
GT = 14
SPAN = 7
GROUPS_COUNTED = 50
LN_EPS = 1e-5


def build(nc, x, src, dst, attr, weight, node_w, review_w, out):
    NODES, F = x.shape
    EDGES = src.shape[0]
    CHUNK = P * TILES
    ALL_CHUNKS = EDGES // CHUNK
    GROUP = GT * P
    COUNTED_FROM = EDGES - GROUPS_COUNTED * GROUP
    CHUNKS = COUNTED_FROM // CHUNK
    PER_PART = TILES // PARTS
    NS = GT * SPAN
    HI = (NODES - 1) // P + 1
    HALF = HI * SPAN // 2
    PAIRS = GROUPS_COUNTED - 2
    ROUNDS = PAIRS // 2
    ALL_ROUNDS = ALL_CHUNKS // SLOTS
    assert EDGES == ALL_CHUNKS * CHUNK and COUNTED_FROM == CHUNKS * CHUNK and 2 * F == P
    assert SLOTS == 4 and CHUNKS == ROUNDS * SLOTS + 1 and ALL_CHUNKS == ALL_ROUNDS * SLOTS + 1
    assert TILES == PARTS * PER_PART and WIN == 1 << WIN_SHIFT and P == 1 << LO_BITS
    assert HI % 2 == 0 and HALF <= 512 and HI * SPAN <= 2048 and NS <= P and ALL_CHUNKS <= P
    MAX_WINDOWS = (NODES - 1) // WIN + 1
    ALL_WINDOWS = MAX_WINDOWS * ALL_CHUNKS

    J = 8
    blocks = [(b * P * J, P, J) for b in range(NODES // (P * J))]
    rest = NODES - len(blocks) * P * J
    if rest:
        j = next(j for j in range(1, J + 1) if rest % j == 0 and rest // j <= P)
        blocks.append((NODES - rest, rest // j, j))
    BLOCKS = len(blocks)

    with ExitStack() as ctx:
        def sb(name, shape, dt=F32):
            return ctx.enter_context(nc.sbuf_tensor(name, shape, dt))

        def ps(name, shape, dt=F32):
            return ctx.enter_context(nc.psum_tensor(name, shape, dt))

        def sem(name):
            return ctx.enter_context(nc.semaphore(name))

        sums = sb("sums", [P, NODES + WIN])
        rows = sb("rows", [P, SLOTS, TILES, 2 * F])
        src_sb = [sb(f"src{s}", [P, TILES], I32) for s in range(SLOTS)]
        dst_sb = [sb(f"dst{s}", [P, TILES], I32) for s in range(SLOTS)]
        w_sb = [sb(f"w{s}", [P, TILES]) for s in range(SLOTS)]
        dst_left = sb("dst_left", [P, TILES])
        scatter = sb("scatter", [P, TILES, WIN])
        x_tab = sb("x_tab", [P, HI, F])
        counts = sb("counts", [P, HI, NS])
        g_idx = [sb(f"g_idx{b}", [GT, 2, P], I32) for b in range(2)]
        g_w = [sb(f"g_w{b}", [GT, P]) for b in range(2)]
        g_attr = [sb(f"g_attr{b}", [P, GT, F]) for b in range(2)]
        hi_lo = sb("hi_lo", [GT, 2, P], I32)
        tile_first = sb("tile_first", [GT, 1])
        w_cut = sb("w_cut", [GT, 2, P], BF16)
        KEY, LO, W1, W2, REL, W0 = range(6)
        packed = sb("packed", [GT, W0, P])
        cols = [sb(f"cols{b}", [P, W0 + 1, GT]) for b in range(2)]
        slot_rel = [sb(f"slot_rel{b}", [NS, 1]) for b in range(2)]
        slot_no = sb("slot_no", [NS, 1])
        spread = sb("spread", [GT, NS])
        hot_key = [sb(f"hot_key{b}", [P, HI * SPAN], BF16) for b in range(2)]
        hot_lo = [sb(f"hot_lo{b}", [P, 3, P], BF16) for b in range(2)]
        hot_rel = [sb(f"hot_rel{b}", [P, SPAN]) for b in range(2)]
        x_sums = sb("x_sums", [P, NS])
        attr_sums = sb("attr_sums", [F, NS])
        fold = sb("fold", [P, F])
        slot_rows = sb("slot_rows", [NS, 2 * F])
        slot_scatter = sb("slot_scatter", [NS, WIN])
        column = sb("column", [P, WIN])
        count16 = sb("count16", [P, HI * SPAN], F16)
        ident = sb("ident", [P, P])
        ones = sb("ones", [P, P])
        eps = sb("eps", [P, 1])
        lo_all = sb("lo_all", [P, ALL_CHUNKS])
        base_tab = sb("base_tab", [1, ALL_CHUNKS], I32)
        window_tab = sb("window_tab", [1, ALL_CHUNKS + 1], I32)
        group_tab = sb("group_tab", [1, GROUPS_COUNTED], I32)
        narrow_tab = sb("narrow_tab", [1, 1], I32)
        early = counts[:, :, :].rearrange("p h n -> p (h n)")

        def early_part(at, np_, shape, dt=F32):
            size = 1
            for n in shape:
                size *= n
            flat = early[0:np_, at:at + size]
            flat = flat.bitcast(dt) if dt != F32 else flat
            return at + size, flat.rearrange("p (a b) -> p a b", a=shape[0])

        at, dst_i = early_part(0, P, [ALL_CHUNKS, TILES], I32)
        at, lo_hi = early_part(at, P, [2, ALL_CHUNKS])
        at, lo_diag = early_part(at, ALL_CHUNKS, [1, ALL_CHUNKS])
        at, lo_hi_col = early_part(at, ALL_CHUNKS, [1, 2])
        at, lo_hi_row = early_part(at, 1, [2, ALL_CHUNKS])
        at, windows_i = early_part(at, 1, [2, ALL_CHUNKS], I32)
        at, windows_f = early_part(at, 1, [2, ALL_CHUNKS])
        at, g_dst = early_part(at, GROUPS_COUNTED, [GT, P], I32)
        at, g_lo_hi = early_part(at, GROUPS_COUNTED, [2, GT])
        at, g_wide = early_part(at, GROUPS_COUNTED, [2, GT])
        at, g_bad = early_part(at, GROUPS_COUNTED, [1, 8])
        at, slot_far = early_part(at, NS, [2, GT])
        at, g_row = early_part(at, 1, [1, GROUPS_COUNTED])
        at, g_worst = early_part(at, 1, [1, 2])
        assert at <= HI * NS
        w_both = sb("w_both", [F, 2 * F])
        w_t = sb("w_t", [2 * F, F])
        nodes = rows[:, 1:SLOTS, :, :].rearrange("p s k f -> p (s k f)")[:, 0:BLOCKS * J * F].rearrange(
            "p (b j f) -> p b j f", b=BLOCKS, j=J)
        square = scatter[:, :, :].rearrange("p k w -> p (k w)")[:, 0:2 * J * F].rearrange(
            "p (b j f) -> p b j f", b=2, j=J)
        mean = sb("mean", [P, BLOCKS, J])
        var = sb("var", [P, BLOCKS, J])
        std = sb("std", [P, BLOCKS, J])
        rstd = sb("rstd", [P, BLOCKS, J])

        window_ps = ps("window_ps", [P, 512])
        count_ps = [ps(f"count_ps{b}", [P, 2, 512]) for b in range(2)]
        x_sums_ps = ps("x_sums_ps", [P, 512])
        attr_ps = ps("attr_ps", [P, 512])
        turn_ps = ps("turn_ps", [P, 512])
        table_ps, row_ps, w_t_ps = count_ps[0][:, 0, :], count_ps[0][:, 1, :], count_ps[1][:, 1, :]
        out_ps = [count_ps[1][:, b, :].rearrange("p (j f) -> p j f", j=J) for b in range(2)]
        slot_rows_ps = x_sums_ps[0:NS, P:P + 2 * F]
        slot_window_ps = turn_ps[:, 256:256 + WIN]
        REL_COL = (W0 + 1) * GT

        dst_loaded = sem("dst_loaded")
        g_dst_loaded = sem("g_dst_loaded")
        w_loaded = sem("w_loaded")
        x_tab_loaded = sem("x_tab_loaded")
        nodes_loaded = sem("nodes_loaded")
        pool_made = sem("pool_made")
        consts_ready = sem("consts_ready")
        dve_step = sem("dve_step")
        lo_hi_ready = sem("lo_hi_ready")
        lo_hi_turned = sem("lo_hi_turned")
        col_ready = sem("col_ready")
        diag_ready = sem("diag_ready")
        rows_turned = sem("rows_turned")
        tables_ready = sem("tables_ready")
        w_turned = sem("w_turned")
        w_t_ready = sem("w_t_ready")
        src_landed = [sem(f"src_landed{s}") for s in range(SLOTS)]
        edge_landed = [sem(f"edge_landed{s}") for s in range(SLOTS)]
        gathers_begun = sem("gathers_begun")
        gathered = [sem(f"gathered{s}") for s in range(SLOTS)]
        slot_free = [sem(f"slot_free{s}") for s in range(SLOTS)]
        scatter_ready = [sem(f"scatter_ready{q}") for q in range(PARTS)]
        window_summed = sem("window_summed")
        window_added = sem("window_added")
        left_ready = sem("left_ready")
        g_landed = [sem(f"g_landed{b}") for b in range(2)]
        prepared = sem("prepared")
        prep_step = sem("prep_step")
        turned = sem("turned")
        cols_ready = sem("cols_ready")
        hot_ready = sem("hot_ready")
        counted = sem("counted")
        counts_read = sem("counts_read")
        attr_read = sem("attr_read")
        x_summed = sem("x_summed")
        x_read = sem("x_read")
        slots_turned = sem("slots_turned")
        slots_read = sem("slots_read")
        slots_hot = sem("slots_hot")
        slots_multiplied = sem("slots_multiplied")
        slots_added = sem("slots_added")
        sums_ready = sem("sums_ready")
        out_multiplied = sem("out_multiplied")
        out_added = sem("out_added")
        mean_ready = sem("mean_ready")
        centred = sem("centred")
        squared = sem("squared")
        var_ready = sem("var_ready")
        std_ready = sem("std_ready")
        rstd_ready = sem("rstd_ready")
        scaled = sem("scaled")
        stored = sem("stored")

        block = ctx.enter_context(nc.Block())

        def by_partition(dram, c):
            return dram[bass.ds(c * CHUNK, CHUNK)].rearrange("(p k) -> p k", k=TILES)

        def by_tile(dram, g):
            return dram[bass.ds(COUNTED_FROM + g * GROUP, GROUP)].rearrange("(t e) -> t e", e=P)

        weights = weight.rearrange("e a -> (e a)")

        def is_narrow(eng):
            return eng.value_load(narrow_tab[0:1, 0:1], min_val=0, max_val=1)

        @block.sync
        def _(sp):
            def load_chunk(c, s, r):
                sp.wait_ge(slot_free[s], r + 1)
                sp.dma_start(src_sb[s][:, :], by_partition(src, c)).then_inc(src_landed[s], 16)
                sp.dma_start(dst_sb[s][:, :], by_partition(dst, c)).then_inc(edge_landed[s], 16)
                sp.dma_start(w_sb[s][:, :], by_partition(weights, c)).then_inc(edge_landed[s], 16)
                sp.dma_start(rows[:, s, :, F:2 * F],
                             attr[bass.ds(c * CHUNK, CHUNK), :].rearrange("(p k) f -> p k f", k=TILES)
                             ).then_inc(edge_landed[s], 16)

            sp.dma_start(dst_i, dst.rearrange("(c p k) -> p c k", p=P, k=TILES)).then_inc(dst_loaded, 16)
            sp.dma_start(g_dst, dst[COUNTED_FROM:EDGES].rearrange("(g t e) -> g t e", t=GT, e=P)
                         ).then_inc(g_dst_loaded, 16)
            sp.dma_start(w_both[:, 0:F], node_w).then_inc(w_loaded, 16)
            sp.dma_start(w_both[:, F:2 * F], review_w).then_inc(w_loaded, 16)
            with sp.Fori(0, ROUNDS) as r:
                for s in range(SLOTS):
                    load_chunk(r * SLOTS + s, s, r)
            load_chunk(CHUNKS - 1, 0, ROUNDS)
            sp.wait_ge(tables_ready, 1)
            with sp.If(is_narrow(sp) == 0):
                with sp.Fori(ROUNDS, ALL_ROUNDS) as r:
                    for s in range(SLOTS):
                        load_chunk(r * SLOTS + 1 + s, (s + 1) % SLOTS, r + (s + 1) // SLOTS)
            sp.wait_ge(sums_ready, 1)
            for b, (n0, np_, j) in enumerate(blocks):
                sp.dma_start(nodes[0:np_, b, 0:j, :],
                             x[n0:n0 + np_ * j, :].rearrange("(p j) f -> p j f", j=j)).then_inc(nodes_loaded, 16)
            for b, (n0, np_, j) in enumerate(blocks):
                sp.wait_ge(scaled, b + 1)
                sp.dma_start(out[n0:n0 + np_ * j, :].rearrange("(p j) f -> p j f", j=j),
                             nodes[0:np_, b, 0:j, :]).then_inc(stored, 16)
            sp.wait_ge(stored, 16 * BLOCKS)

        @block.gpsimd
        def _(pool):
            def gather_chunk(s, r):
                pool.wait_ge(src_landed[s], (r + 1) * 16)
                pool.wait_ge(slot_free[s], r + 1)
                pool.sem_inc(gathers_begun, 1)
                for k in range(TILES):
                    pool.indirect_dma_start(
                        out=rows[:, s, k, 0:F], out_offset=None, in_=x,
                        in_offset=bass.IndirectOffsetOnAxis(ap=src_sb[s][:, k:k + 1].bitcast(U32), axis=0),
                    ).then_inc(gathered[s], 16)

            def scale_rows(b):
                n0, np_, j = blocks[b]
                y = nodes[0:np_, b, 0:j, :]
                pool.wait_ge(rstd_ready, b + 1)
                pool.wait_ge(squared, b + 1)
                pool.wait_ge(centred, b + 1)
                pool.tensor_tensor(y, y, rstd[0:np_, b, 0:j].unsqueeze(2).to_broadcast([np_, j, F]), ALU.mult
                                   ).then_inc(scaled, 1)

            pool.memset(ident[:, :], 0.0).then_inc(pool_made, 1)
            pool.memset(spread[:, :], 1.0).then_inc(pool_made, 1)
            pool.memset(fold[:, :], 0.0).then_inc(pool_made, 1)
            pool.iota(count16[:, :], pattern=[[1, HI * SPAN]], base=0, channel_multiplier=0,
                      allow_small_or_imprecise_dtypes=True).then_inc(pool_made, 1)
            pool.iota(column[:, :], pattern=[[1, WIN]], base=0, channel_multiplier=0,
                      allow_small_or_imprecise_dtypes=True).then_inc(pool_made, 1)
            pool.iota(slot_far[:, 0, :], pattern=[[-SPAN, GT]], base=0, channel_multiplier=1,
                      allow_small_or_imprecise_dtypes=True).then_inc(pool_made, 1)
            pool.wait_ge(pool_made, 6)
            pool.affine_select(out=ident[:, :], in_=ident[:, :], compare_op=ALU.not_equal, fill=1.0,
                               base=0, pattern=[[-1, P]], channel_multiplier=1).then_inc(pool_made, 1)
            pool.affine_select(out=fold[:, :], in_=fold[:, :], compare_op=ALU.not_equal, fill=1.0,
                               base=0, pattern=[[-1, F]], channel_multiplier=1).then_inc(pool_made, 1)
            pool.affine_select(out=spread[:, :], in_=spread[:, :], compare_op=ALU.is_ge, fill=0.0,
                               base=0, pattern=[[1, NS]], channel_multiplier=-SPAN).then_inc(pool_made, 1)
            pool.wait_ge(pool_made, 9)
            pool.affine_select(out=fold[:, :], in_=fold[:, :], compare_op=ALU.not_equal, fill=1.0,
                               base=-F, pattern=[[-1, F]], channel_multiplier=1).then_inc(pool_made, 1)
            pool.affine_select(out=spread[:, :], in_=spread[:, :], compare_op=ALU.is_ge, fill=0.0,
                               base=SPAN - 1, pattern=[[-1, NS]], channel_multiplier=SPAN).then_inc(pool_made, 1)

            with pool.Fori(0, ROUNDS) as r:
                for s in range(SLOTS):
                    gather_chunk(s, r)
            gather_chunk(0, ROUNDS)
            pool.wait_ge(tables_ready, 1)
            with pool.If(is_narrow(pool) == 0):
                with pool.Fori(ROUNDS, ALL_ROUNDS) as r:
                    for s in range(SLOTS):
                        gather_chunk((s + 1) % SLOTS, r + (s + 1) // SLOTS)
            for b, (n0, np_, j) in enumerate(blocks):
                y = nodes[0:np_, b, 0:j, :]
                pool.wait_ge(mean_ready, b + 1)
                pool.tensor_tensor(y, y, mean[0:np_, b, 0:j].unsqueeze(2).to_broadcast([np_, j, F]), ALU.subtract
                                   ).then_inc(centred, 1)
                if b >= 1:
                    scale_rows(b - 1)
            scale_rows(BLOCKS - 1)

        @block.vector
        def _(dve):
            steps = 0

            def step(ins):
                nonlocal steps
                steps += 1
                ins.then_inc(dve_step, 1)
                dve.wait_ge(dve_step, steps)

            def add_chunk(c, s, r):
                base = dve.value_load(base_tab[0:1, bass.ds(c, 1)], min_val=0, max_val=NODES - 1)
                first = dve.value_load(window_tab[0:1, bass.ds(c, 1)], min_val=0, max_val=ALL_WINDOWS)
                until = dve.value_load(window_tab[0:1, bass.ds(c + 1, 1)], min_val=0, max_val=ALL_WINDOWS)
                dve.wait_ge(edge_landed[s], (r + 1) * 48)
                dve.wait_ge(left_ready, first + c + 1)
                dve.tensor_scalar(dst_left[:, :], dst_sb[s][:, :], lo_all[:, bass.ds(c, 1)], None, ALU.subtract
                                  ).then_inc(left_ready, 1)
                with dve.Fori(first, until) as w:
                    dve.wait_ge(left_ready, w + c + 2)
                    for q in range(PARTS):
                        for k in range(q * PER_PART, (q + 1) * PER_PART):
                            made = dve.tensor_scalar(scatter[:, k, :], column[:, :], dst_left[:, k:k + 1],
                                                     w_sb[s][:, k:k + 1], ALU.is_equal, ALU.mult)
                        made.then_inc(scatter_ready[q], 1)
                    dve.wait_ge(window_summed, w + 1)
                    dve.wait_ge(window_added, w + 1)
                    dve.tensor_scalar(dst_left[:, :], dst_left[:, :], float(WIN), None, ALU.subtract
                                      ).then_inc(left_ready, 1)
                    to = nc.s_assert_within(
                        base + (w - first) * WIN, 0, NODES - 1, skip_runtime_bounds_check_because=
                        "a chunk's last window begins at or before its largest dst, which is a node")
                    dve.tensor_tensor(sums[:, bass.ds(to, WIN)], sums[:, bass.ds(to, WIN)],
                                      window_ps[:, 0:WIN], ALU.add).then_inc(window_added, 1)
                dve.sem_inc(slot_free[s], 1)
                return until

            def prepare(g, b, n):
                dve.wait_ge(g_landed[b], n * 64)
                if not (isinstance(g, int) and g == 0):
                    dve.wait_ge(turned, g)
                src_i, dst_i, w_i = g_idx[b][:, 0, :], g_idx[b][:, 1, :], g_w[b][:, :]
                dve.tensor_reduce(tile_first[:, :], dst_i, AX_X, ALU.min).then_inc(prep_step, 1)
                dve.tensor_scalar(hi_lo[:, 0, :], src_i, LO_BITS, None, ALU.arith_shift_right)
                dve.tensor_scalar(hi_lo[:, 1, :], src_i, P - 1, None, ALU.bitwise_and)
                dve.tensor_copy(w_cut[:, 0, :], w_i).then_inc(prep_step, 1)
                dve.wait_ge(prep_step, 5 * g + 2)
                dve.tensor_scalar(packed[:, REL, :], dst_i, tile_first[:, 0:1], None, ALU.subtract)
                dve.tensor_tensor(packed[:, W1, :], w_i, w_cut[:, 0, :], ALU.subtract).then_inc(prep_step, 1)
                dve.wait_ge(prep_step, 5 * g + 3)
                dve.tensor_copy(w_cut[:, 1, :], packed[:, W1, :]).then_inc(prep_step, 1)
                dve.scalar_tensor_tensor(packed[:, KEY, :], hi_lo[:, 0, :], float(SPAN), packed[:, REL, :],
                                         ALU.mult, ALU.add)
                dve.tensor_copy(packed[:, LO, :], hi_lo[:, 1, :]).then_inc(prep_step, 1)
                dve.wait_ge(prep_step, 5 * g + 5)
                dve.tensor_tensor(packed[:, W2, :], packed[:, W1, :], w_cut[:, 1, :], ALU.subtract
                                  ).then_inc(prepared, 1)

            def make_hot(g, b):
                dve.wait_ge(cols_ready, g + 1)
                for t in range(GT):
                    h = t % 2
                    if not (isinstance(g, int) and g * GT + t < 2):
                        dve.wait_ge(counted, g * GT + t - 1)
                    dve.tensor_scalar(hot_key[h][:, :], count16[:, :], cols[b][:, KEY, t:t + 1], None, ALU.is_equal)
                    for i, part in enumerate((W0, W1, W2)):
                        dve.tensor_scalar(hot_lo[h][:, i, :], count16[:, 0:P], cols[b][:, LO, t:t + 1],
                                          cols[b][:, part, t:t + 1], ALU.is_equal, ALU.mult)
                    dve.tensor_scalar(hot_rel[h][:, :], column[:, 0:SPAN], cols[b][:, REL, t:t + 1],
                                      cols[b][:, W0, t:t + 1], ALU.is_equal, ALU.mult).then_inc(hot_ready, 1)

            def make_slots_hot(g, b):
                dve.wait_ge(cols_ready, g + 1)
                dve.tensor_scalar(slot_scatter[:, :], column[0:NS, :], slot_rel[b][:, 0:1], None, ALU.is_equal
                                  ).then_inc(slots_hot, 1)

            def add_slots(g, until):
                base = dve.value_load(group_tab[0:1, bass.ds(g, 1)], min_val=0, max_val=NODES - 1)
                dve.wait_ge(window_added, until + 1)
                dve.wait_ge(slots_multiplied, g + 1)
                dve.tensor_tensor(sums[:, bass.ds(base, WIN)], sums[:, bass.ds(base, WIN)],
                                  slot_window_ps, ALU.add).then_inc(slots_added, 1)
                dve.wait_ge(slots_added, g + 1)

            for s in range(SLOTS):
                dve.sem_inc(slot_free[s], 1)
            dve.memset(ones[:, :], 1.0)
            dve.memset(eps[:, :], LN_EPS)
            dve.memset(x_tab[:, HI - 1, :], 0.0).then_inc(consts_ready, 1)
            dve.wait_ge(pool_made, 11)
            step(dve.tensor_scalar(slot_far[:, 1, :], slot_far[:, 0, :], 0.0, float(P), ALU.is_lt, ALU.mult))
            step(dve.scalar_tensor_tensor(slot_far[:, 1, :], slot_far[:, 1, :], float(P), slot_far[:, 0, :],
                                          ALU.mult, ALU.add))
            dve.tensor_reduce(slot_no[:, :], slot_far[:, 1, :], AX_X, ALU.min)
            dve.tensor_scalar(spread[0:1, :], spread[0:1, :], 1.0, None, ALU.subtract)
            dve.wait_ge(dst_loaded, 16)
            dve.tensor_reduce(lo_hi[:, 0, :], dst_i, AX_X, ALU.min)
            dve.tensor_reduce(lo_hi[:, 1, :], dst_i, AX_X, ALU.max).then_inc(lo_hi_ready, 1)
            dve.wait_ge(g_dst_loaded, 16)
            dve.tensor_reduce(g_lo_hi[:, 0, :], g_dst, AX_X, ALU.min)
            step(dve.tensor_reduce(g_lo_hi[:, 1, :], g_dst, AX_X, ALU.max))
            dve.tensor_tensor(g_wide[:, 0, :], g_lo_hi[:, 1, :], g_lo_hi[:, 0, :], ALU.subtract)
            step(dve.tensor_scalar(g_wide[:, 1, :], g_lo_hi[:, 0, :], g_lo_hi[:, 0, 0:1], None, ALU.subtract))
            dve.tensor_reduce(g_bad[:, 0, 0:1], g_wide[:, 0, :], AX_X, ALU.max)
            dve.tensor_reduce(g_bad[:, 0, 1:2], g_wide[:, 1, :], AX_X, ALU.max)
            step(dve.tensor_reduce(g_bad[:, 0, 2:3], g_wide[:, 1, :], AX_X, ALU.min))
            dve.tensor_scalar(g_bad[:, 0, 3:4], g_bad[:, 0, 0:1], float(SPAN), None, ALU.is_ge)
            dve.tensor_scalar(g_bad[:, 0, 4:5], g_bad[:, 0, 1:2], float(WIN - SPAN + 1), None, ALU.is_ge)
            step(dve.tensor_scalar(g_bad[:, 0, 5:6], g_bad[:, 0, 2:3], 0.0, None, ALU.is_lt))
            step(dve.tensor_tensor(g_bad[:, 0, 6:7], g_bad[:, 0, 3:4], g_bad[:, 0, 4:5], ALU.add))
            dve.tensor_tensor(g_bad[:, 0, 7:8], g_bad[:, 0, 6:7], g_bad[:, 0, 5:6], ALU.add).then_inc(col_ready, 1)
            dve.wait_ge(lo_hi_turned, 1)
            dve.tensor_reduce(lo_hi_col[:, 0, 0:1], table_ps[0:ALL_CHUNKS, 0:P], AX_X, ALU.min)
            dve.tensor_reduce(lo_hi_col[:, 0, 1:2], table_ps[0:ALL_CHUNKS, P:2 * P], AX_X, ALU.max
                              ).then_inc(col_ready, 1)
            dve.wait_ge(col_ready, 2)
            dve.tensor_scalar(lo_diag[:, 0, :], ident[0:ALL_CHUNKS, 0:ALL_CHUNKS], lo_hi_col[:, 0, 0:1], None, ALU.mult
                              ).then_inc(diag_ready, 1)
            dve.wait_ge(rows_turned, 1)
            dve.tensor_copy(lo_hi_row, row_ps[0:1, 0:2 * ALL_CHUNKS].rearrange("p (a c) -> p a c", a=2))
            dve.tensor_copy(g_row[:, 0, :], row_ps[0:1, 256:256 + GROUPS_COUNTED])
            dve.tensor_copy(group_tab[:, :], row_ps[0:1, 320:320 + GROUPS_COUNTED])
            step(dve.tensor_copy(lo_all[:, :], table_ps[:, 2 * P:2 * P + ALL_CHUNKS]))
            dve.tensor_copy(base_tab[0:1, :], lo_hi_row[:, 0, :])
            step(dve.tensor_tensor(windows_i[:, 0, :], lo_hi_row[:, 1, :], lo_hi_row[:, 0, :], ALU.subtract))
            step(dve.tensor_scalar(windows_i[:, 1, :], windows_i[:, 0, :], WIN_SHIFT, None, ALU.arith_shift_right))
            step(dve.tensor_scalar(windows_f[:, 0, :], windows_i[:, 1, :], 1.0, None, ALU.add))
            step(dve.tensor_tensor_scan(windows_f[:, 1, :], ones[0:1, 0:ALL_CHUNKS], windows_f[:, 0, :], 0.0,
                                        ALU.mult, ALU.add))
            dve.memset(window_tab[:, 0:1], 0)
            dve.tensor_copy(window_tab[:, 1:ALL_CHUNKS + 1], windows_f[:, 1, :])
            step(dve.tensor_reduce(g_worst[:, 0, 0:1], g_row[:, 0, :], AX_X, ALU.max))
            dve.tensor_scalar(narrow_tab[:, :], g_worst[:, 0, 0:1], 0.0, None, ALU.is_equal).then_inc(tables_ready, 1)
            dve.memset(sums[:, :], 0.0).then_inc(window_added, 1)
            dve.wait_ge(w_turned, 1)
            dve.tensor_copy(w_t[:, :], w_t_ps[:, 0:F]).then_inc(w_t_ready, 1)
            dve.wait_ge(tables_ready, 1)
            dve.sem_inc(left_ready, 1)
            narrow = is_narrow(dve)
            with dve.If(narrow == 1):
                prepare(0, 0, 1)
                make_hot(0, 0)
                prepare(1, 1, 1)
                with dve.Fori(0, ROUNDS) as r:
                    for u in range(2):
                        g, b = r * 2 + u + 1, (u + 1) % 2
                        add_chunk(r * SLOTS + 2 * u, 2 * u, r)
                        make_hot(g, b)
                        until = add_chunk(r * SLOTS + 2 * u + 1, 2 * u + 1, r)
                        make_slots_hot(g - 1, 1 - b)
                        prepare(g + 1, 1 - b, r + 2)
                        add_slots(g - 1, until)
                last = GROUPS_COUNTED - 1
                until = add_chunk(CHUNKS - 1, 0, ROUNDS)
                make_hot(last, last % 2)
                make_slots_hot(last - 1, (last - 1) % 2)
                add_slots(last - 1, until)
                make_slots_hot(last, last % 2)
                add_slots(last, until)
                dve.sem_inc(sums_ready, 1)
            with dve.Else():
                with dve.Fori(0, ALL_ROUNDS) as r:
                    for s in range(SLOTS):
                        add_chunk(r * SLOTS + s, s, r)
                until = add_chunk(ALL_CHUNKS - 1, 0, ALL_ROUNDS)
                dve.wait_ge(window_added, until + 1)
                dve.sem_inc(sums_ready, 1)

            dve.wait_ge(nodes_loaded, 16 * BLOCKS)
            for b in range(BLOCKS + 1):
                if b < BLOCKS:
                    n0, np_, j = blocks[b]
                    y = nodes[0:np_, b, 0:j, :]
                    dve.wait_ge(out_multiplied, b + 1)
                    dve.tensor_tensor(y, y, out_ps[b % 2][0:np_, 0:j, :], ALU.add).then_inc(out_added, 1)
                    dve.wait_ge(out_added, b + 1)
                    step(dve.tensor_reduce(mean[0:np_, b, 0:j], y, AX_X, ALU.add))
                    dve.tensor_scalar(mean[0:np_, b, 0:j], mean[0:np_, b, 0:j], 1.0 / F, None, ALU.mult
                                      ).then_inc(mean_ready, 1)
                if b >= 1:
                    n0, np_, j = blocks[b - 1]
                    dve.wait_ge(squared, b)
                    dve.tensor_reduce(var[0:np_, b - 1, 0:j], square[0:np_, (b - 1) % 2, 0:j, :], AX_X, ALU.add
                                      ).then_inc(var_ready, 1)
                    dve.wait_ge(std_ready, b)
                    dve.reciprocal(rstd[0:np_, b - 1, 0:j], std[0:np_, b - 1, 0:j]).then_inc(rstd_ready, 1)

        @block.scalar
        def _(act):
            def load_group(g, b, first):
                if not first:
                    act.wait_ge(counted, (g - 1) * GT)
                    act.wait_ge(turned, g - 1)
                    act.wait_ge(prepared, g - 1)
                act.dma_start(g_idx[b][:, 0, :], by_tile(src, g)).then_inc(g_landed[b], 16)
                act.dma_start(g_idx[b][:, 1, :], by_tile(dst, g)).then_inc(g_landed[b], 16)
                act.dma_start(g_w[b][:, :], by_tile(weights, g)).then_inc(g_landed[b], 16)
                act.dma_start(g_attr[b][:, :, :],
                              attr[bass.ds(COUNTED_FROM + g * GROUP, GROUP), :].rearrange("(t e) f -> e t f", e=P)
                              ).then_inc(g_landed[b], 16)

            def read_cols(g, b):
                act.wait_ge(turned, g + 1)
                if not isinstance(g, int) or g >= 2:
                    act.wait_ge(slots_hot, g - 1)
                act.activation(slot_rel[b][:, :], turn_ps[0:NS, REL_COL:REL_COL + 1], ACT.Identity, bias=slot_no[:, 0:1])
                act.activation(cols[b][:, :, :], turn_ps[:, 0:REL_COL].rearrange("p (q t) -> p q t", t=GT), ACT.Copy
                               ).then_inc(cols_ready, 1)

            def read_slots(g):
                act.wait_ge(slots_turned, g + 1)
                act.activation(slot_rows[:, :], slot_rows_ps, ACT.Copy).then_inc(slots_read, 1)

            def read_counts(g):
                for t in range(GT):
                    act.wait_ge(counted, g * GT + t + 1)
                    if t == 0 and not (isinstance(g, int) and g == 0):
                        act.wait_ge(x_summed, g)
                    act.activation(
                        counts[:, :, t * SPAN:(t + 1) * SPAN].rearrange("p (a h) d -> p a h d", a=2),
                        count_ps[t % 2][:, :, 0:HALF].rearrange("p a (h d) -> p a h d", d=SPAN), ACT.Copy
                    ).then_inc(counts_read, 1)
                act.activation(attr_sums[:, :], attr_ps[0:F, 0:NS], ACT.Copy).then_inc(attr_read, 1)

            def read_x_sums(g):
                act.wait_ge(x_summed, g + 1)
                act.activation(x_sums[:, :], x_sums_ps[:, 0:NS], ACT.Copy).then_inc(x_read, 1)

            act.wait_ge(consts_ready, 1)
            FULL = NODES // P
            act.dma_start(x_tab[:, 0:FULL, :], x[0:FULL * P, :].rearrange("(h l) f -> l h f", l=P)
                          ).then_inc(x_tab_loaded, 16)
            if FULL < HI:
                act.dma_start(x_tab[0:NODES - FULL * P, FULL, :], x[FULL * P:NODES, :]).then_inc(x_tab_loaded, 16)
            act.wait_ge(tables_ready, 1)
            with act.If(is_narrow(act) == 1):
                load_group(0, 0, True)
                load_group(1, 1, True)
                read_cols(0, 0)
                read_counts(0)
                read_x_sums(0)
                with act.Fori(0, ROUNDS) as r:
                    for u in range(2):
                        g, b = r * 2 + u + 1, (u + 1) % 2
                        read_cols(g, b)
                        load_group(g + 1, 1 - b, False)
                        read_slots(g - 1)
                        read_counts(g)
                        read_x_sums(g)
                last = GROUPS_COUNTED - 1
                read_cols(last, last % 2)
                read_slots(last - 1)
                read_counts(last)
                read_x_sums(last)
                read_slots(last)
            for b in range(BLOCKS):
                n0, np_, j = blocks[b]
                act.wait_ge(centred, b + 1)
                if b >= 2:
                    act.wait_ge(var_ready, b - 1)
                act.activation(square[0:np_, b % 2, 0:j, :], nodes[0:np_, b, 0:j, :], ACT.Square).then_inc(squared, 1)
                act.wait_ge(var_ready, b + 1)
                act.activation(std[0:np_, b, 0:j], var[0:np_, b, 0:j], ACT.Sqrt, bias=eps[0:np_, :], scale=1.0 / F
                               ).then_inc(std_ready, 1)

        @block.tensor
        def _(pe):
            def sum_chunk(c, s, r):
                first = pe.value_load(window_tab[0:1, bass.ds(c, 1)], min_val=0, max_val=ALL_WINDOWS)
                until = pe.value_load(window_tab[0:1, bass.ds(c + 1, 1)], min_val=0, max_val=ALL_WINDOWS)
                with pe.Fori(first, until) as w:
                    pe.wait_ge(edge_landed[s], (r + 1) * 48)
                    pe.wait_ge(gathered[s], (r + 1) * (16 * TILES))
                    pe.wait_ge(window_added, w + 1)
                    for k in range(TILES):
                        if k % PER_PART == 0:
                            pe.wait_ge(scatter_ready[k // PER_PART], w + 1)
                        done = pe.matmul(window_ps[:, 0:WIN], rows[:, s, k, :], scatter[:, k, :],
                                         start=(k == 0), stop=(k == TILES - 1))
                    done.then_inc(window_summed, 1)

            def turn_cols(g, b):
                pe.wait_ge(prepared, g + 1)
                if not isinstance(g, int) or g >= 2:
                    pe.wait_ge(slots_added, g - 1)
                if not isinstance(g, int) or g >= 1:
                    pe.wait_ge(cols_ready, g)
                pe.matmul(turn_ps[0:NS, REL_COL:REL_COL + 1], spread[:, :], tile_first[:, 0:1], start=True, stop=True)
                for q in range(W0):
                    pe.transpose(turn_ps[:, q * GT:(q + 1) * GT], packed[:, q, :], ident[0:GT, 0:GT])
                pe.transpose(turn_ps[:, W0 * GT:(W0 + 1) * GT], g_w[b][:, :], ident[0:GT, 0:GT]).then_inc(turned, 1)

            def count_tiles(g, b, n):
                pe.wait_ge(g_landed[b], n * 64)
                if not isinstance(g, int) or g >= 1:
                    pe.wait_ge(attr_read, g)
                for t in range(GT):
                    h = t % 2
                    pe.wait_ge(hot_ready, g * GT + t + 1)
                    if not (isinstance(g, int) and g * GT + t < 2):
                        pe.wait_ge(counts_read, g * GT + t - 1)
                    for i in range(3):
                        for a in range(2):
                            pe.matmul(count_ps[h][:, a, 0:HALF], hot_lo[h][:, i, :],
                                      hot_key[h][:, a * HALF:(a + 1) * HALF], start=(i == 0), stop=(i == 2))
                    pe.matmul(attr_ps[0:F, t * SPAN:(t + 1) * SPAN], g_attr[b][:, t, :], hot_rel[h][:, :],
                              start=True, stop=True).then_inc(counted, 1)

            def sum_x(g):
                pe.wait_ge(counts_read, (g + 1) * GT)
                if not isinstance(g, int) or g >= 1:
                    pe.wait_ge(slots_read, g)
                for hi in range(HI):
                    half = hi % 2
                    done = pe.matmul(x_sums_ps[half * F:(half + 1) * F, 0:NS], x_tab[:, hi, :], counts[:, hi, :],
                                     start=(hi < 2), stop=(hi >= HI - 2))
                done.then_inc(x_summed, 1)

            def turn_slots(g):
                pe.wait_ge(x_read, g + 1)
                pe.wait_ge(attr_read, g + 1)
                pe.matmul(slot_rows_ps[:, 0:F], x_sums[:, :], fold[:, :], start=True, stop=True)
                pe.matmul(slot_rows_ps[:, F:2 * F], attr_sums[:, :], ident[0:F, 0:F], start=True, stop=True
                          ).then_inc(slots_turned, 1)

            def multiply_slots(g):
                pe.wait_ge(slots_read, g + 1)
                pe.wait_ge(slots_hot, g + 1)
                pe.matmul(slot_window_ps, slot_rows[:, :], slot_scatter[:, :], start=True, stop=True
                          ).then_inc(slots_multiplied, 1)

            pe.wait_ge(pool_made, 11)
            pe.wait_ge(lo_hi_ready, 1)
            pe.transpose(table_ps[0:ALL_CHUNKS, 0:P], lo_hi[:, 0, :], ident[:, :])
            pe.transpose(table_ps[0:ALL_CHUNKS, P:2 * P], lo_hi[:, 1, :], ident[:, :]).then_inc(lo_hi_turned, 1)
            pe.wait_ge(col_ready, 2)
            for a in range(2):
                pe.matmul(row_ps[0:1, a * ALL_CHUNKS:(a + 1) * ALL_CHUNKS], lo_hi_col[:, 0, a:a + 1],
                          ident[0:ALL_CHUNKS, 0:ALL_CHUNKS], start=True, stop=True)
            for at_, col in ((256, g_bad[:, 0, 7:8]), (320, g_lo_hi[:, 0, 0:1])):
                pe.matmul(row_ps[0:1, at_:at_ + GROUPS_COUNTED], col, ident[0:GROUPS_COUNTED, 0:GROUPS_COUNTED],
                          start=True, stop=True)
            pe.wait_ge(diag_ready, 1)
            pe.matmul(table_ps[:, 2 * P:2 * P + ALL_CHUNKS], ones[0:ALL_CHUNKS, :], lo_diag[:, 0, :],
                      start=True, stop=True).then_inc(rows_turned, 1)
            pe.wait_ge(w_loaded, 32)
            pe.transpose(w_t_ps[:, 0:F], w_both[:, :], ident[0:F, 0:F]).then_inc(w_turned, 1)
            pe.wait_ge(w_t_ready, 1)
            pe.wait_ge(tables_ready, 1)
            with pe.If(is_narrow(pe) == 1):
                pe.wait_ge(x_tab_loaded, 32 if NODES % P else 16)
                turn_cols(0, 0)
                count_tiles(0, 0, 1)
                sum_x(0)
                with pe.Fori(0, ROUNDS) as r:
                    for u in range(2):
                        g, b = r * 2 + u + 1, (u + 1) % 2
                        turn_cols(g, b)
                        sum_chunk(r * SLOTS + 2 * u, 2 * u, r)
                        turn_slots(g - 1)
                        count_tiles(g, b, r + 1 if u == 0 else r + 2)
                        sum_chunk(r * SLOTS + 2 * u + 1, 2 * u + 1, r)
                        multiply_slots(g - 1)
                        sum_x(g)
                last = GROUPS_COUNTED - 1
                turn_cols(last, last % 2)
                sum_chunk(CHUNKS - 1, 0, ROUNDS)
                turn_slots(last - 1)
                count_tiles(last, last % 2, last // 2 + 1)
                multiply_slots(last - 1)
                sum_x(last)
                turn_slots(last)
                multiply_slots(last)
            with pe.Else():
                with pe.Fori(0, ALL_ROUNDS) as r:
                    for s in range(SLOTS):
                        sum_chunk(r * SLOTS + s, s, r)
                sum_chunk(ALL_CHUNKS - 1, 0, ALL_ROUNDS)

            pe.wait_ge(sums_ready, 1)
            for b, (n0, np_, j) in enumerate(blocks):
                if b >= 2:
                    pe.wait_ge(out_added, b - 1)
                for i in range(j):
                    last = pe.matmul(out_ps[b % 2][0:np_, i, :], sums[:, n0 + i:n0 + (np_ - 1) * j + i + 1:j],
                                     w_t[:, :], start=True, stop=True)
                last.then_inc(out_multiplied, 1)


INPUTS = ["x", "src", "dst", "edge_attr_64", "edge_weight1", "L0_gnn_node_w", "L0_gnn_review_w"]


def kernel(**inputs):
    import numpy as np
    import concourse.bacc as bacc
    from concourse.bass_utils import run_bass_kernel_spmd

    nc = bacc.Bacc("TRN2", target_bir_lowering=False, num_devices=1)
    arrays, args = {}, []
    for name in INPUTS:
        a = np.ascontiguousarray(inputs[name])
        arrays[name] = a
        args.append(nc.dram_tensor(name, a.shape, mybir.dt.from_np(a.dtype), kind="ExternalInput").ap())
    out = nc.dram_tensor("out", arrays["x"].shape, F32, kind="ExternalOutput").ap()
    build(nc, *args, out)
    result = run_bass_kernel_spmd(nc, [arrays], core_ids=[0])
    return result.results[0]["out"]
```

```python
from contextlib import ExitStack

import concourse.bass as bass
from concourse import mybir

ALU = mybir.AluOpType
ACT = mybir.ActivationFunctionType
F32 = mybir.dt.float32
F16 = mybir.dt.float16
BF16 = mybir.dt.bfloat16
I32 = mybir.dt.int32
U32 = mybir.dt.uint32
AX_X = mybir.AxisListType.X

P = 128
LO_BITS = 7
TILES = 25
SLOTS = 4
PARTS = 5
PART_BUFS = 3
WIN = 128
WIN_SHIFT = 7
GT = 18
HOT_BUFS = 3
SPAN = 7
CHUNKS = 88
STEPS = (2, 1, 2, 1, 2)
LAST_STEPS = (2, 2, 2, 2, 2, 2)
LATE_CHUNKS = 2
LN_EPS = 1e-5


def build(nc, x, src, dst, attr, weight, node_w, review_w, out):
    NODES, F = x.shape
    EDGES = src.shape[0]
    CHUNK = P * TILES
    ALL_CHUNKS = EDGES // CHUNK
    GROUP = GT * P
    COUNTED_FROM = CHUNKS * CHUNK
    COUNTED = (EDGES - COUNTED_FROM) // P
    GROUPS = (COUNTED - 1) // GT + 1
    GT0 = COUNTED - (GROUPS - 1) * GT
    PER_PART = TILES // PARTS
    NS = GT * SPAN
    HI = (NODES - 1) // P + 1
    HALF = HI * SPAN // 2
    ROUND_CHUNKS, ROUND_GROUPS = sum(STEPS), len(STEPS)
    ROUNDS = (GROUPS - 1 - len(LAST_STEPS)) // ROUND_GROUPS
    last_chunks = list(range(ROUNDS * ROUND_CHUNKS, CHUNKS - LATE_CHUNKS))
    last_steps = [(g, [last_chunks.pop(0) for _ in range(n)])
                  for g, n in enumerate(LAST_STEPS, ROUNDS * ROUND_GROUPS + 1)]
    assert EDGES == ALL_CHUNKS * CHUNK and 2 * F == P and SLOTS == 4 and ROUND_CHUNKS % SLOTS == 0
    assert last_steps[-1][0] == GROUPS - 1 and len(last_steps) >= 2 and last_chunks
    assert GT0 >= HOT_BUFS and GT % HOT_BUFS == 0
    assert TILES == PARTS * PER_PART and WIN == 1 << WIN_SHIFT and P == 1 << LO_BITS
    assert HI % 2 == 0 and HALF <= 512 and HI * SPAN <= 2048 and NS <= P and ALL_CHUNKS <= P
    MAX_WINDOWS = (NODES - 1) // WIN + 1
    ALL_WINDOWS = MAX_WINDOWS * ALL_CHUNKS

    late_rows = range(((CHUNKS - LATE_CHUNKS) * NODES // ALL_CHUNKS - WIN) // P,
                      (CHUNKS * NODES // ALL_CHUNKS + 2 * WIN) // P + 1)
    LATE_NODES = (late_rows[0] * P, (late_rows[-1] + 1) * P)
    J = 8
    middle = late_rows[len(late_rows) // 2]
    edges = sorted({*range(0, late_rows[0], J), late_rows[0], middle, *range(late_rows[-1] + 1, HI, J), HI})
    blocks = [(h, until - h) for h, until in zip(edges, edges[1:])]
    BLOCKS = len(blocks)
    late = [b for b, (h, _) in enumerate(blocks) if h in late_rows]
    early = [b for b in range(BLOCKS) if b not in late]
    ACT_BLOCKS = len(early) // 2 + 1
    assert late_rows[-1] + 1 < NODES // P and late_rows[0] > 0
    BY_P = NODES // P
    G_DST_DMAS = 1 + (GT - 1) // GT0 + 1

    with ExitStack() as ctx:
        def sb(name, shape, dt=F32):
            return ctx.enter_context(nc.sbuf_tensor(name, shape, dt))

        def ps(name, shape, dt=F32):
            return ctx.enter_context(nc.psum_tensor(name, shape, dt))

        def sem(name):
            return ctx.enter_context(nc.semaphore(name))

        sums = sb("sums", [P, NODES + WIN])
        rows = sb("rows", [P, SLOTS, TILES, 2 * F])
        src_sb = [sb(f"src{s}", [P, TILES], I32) for s in range(SLOTS)]
        dst_sb = [sb(f"dst{s}", [P, TILES], I32) for s in range(SLOTS)]
        w_sb = [sb(f"w{s}", [P, TILES]) for s in range(SLOTS)]
        dst_left = sb("dst_left", [P, TILES])
        scatter = sb("scatter", [P, PART_BUFS, PER_PART, WIN])
        x_tab = sb("x_tab", [P, HI, F])
        counts = sb("counts", [P, HI, NS])
        g_idx = sb("g_idx", [GT, 2, P], I32)
        g_w = sb("g_w", [GT, P])
        g_attr = sb("g_attr", [P, GT, F])
        hi_lo = sb("hi_lo", [GT, 2, P], I32)
        tile_first = sb("tile_first", [GT, 1])
        w_cut = sb("w_cut", [GT, 2, P], BF16)
        KEY, LO, W1, W2, REL, W0 = range(6)
        packed = sb("packed", [GT, W0, P])
        cols = sb("cols", [P, W0 + 1, GT])
        slot_rel = sb("slot_rel", [NS, 1])
        slot_no = sb("slot_no", [NS, 1])
        spread = sb("spread", [GT, NS])
        hot_key = [sb(f"hot_key{b}", [P, HI * SPAN], BF16) for b in range(HOT_BUFS)]
        hot_lo = [sb(f"hot_lo{b}", [P, 3, P], BF16) for b in range(HOT_BUFS)]
        hot_rel = sb("hot_rel", [P, GT, SPAN])
        x_sums = sb("x_sums", [P, NS])
        attr_sums = sb("attr_sums", [P, NS])
        fold = sb("fold", [P, F])
        slot_rows = sb("slot_rows", [NS, 2 * F])
        slot_scatter = sb("slot_scatter", [NS, WIN])
        column = sb("column", [P, WIN])
        count16 = sb("count16", [P, HI * SPAN], F16)
        ident = sb("ident", [P, P])
        eps = sb("eps", [P, 1])
        lo_all = sb("lo_all", [P, ALL_CHUNKS])
        base_tab = sb("base_tab", [1, ALL_CHUNKS], I32)
        window_tab = sb("window_tab", [1, ALL_CHUNKS + 1], I32)
        group_tab = sb("group_tab", [1, GROUPS], I32)
        flag_tab = sb("flag_tab", [1, 2], I32)
        room = counts[:, :, :].rearrange("p h n -> p (h n)")

        def part(at, np_, shape, dt=F32):
            size = 1
            for n in shape:
                size *= n
            flat = room[0:np_, at:at + size]
            flat = flat.bitcast(dt) if dt != F32 else flat
            return at + size, flat.rearrange("p (a b) -> p a b", a=shape[0])

        at, dst_i = part(0, ALL_CHUNKS, [1, CHUNK], I32)
        at, ones = part(at, P, [1, P])
        at, lo_diag = part(at, ALL_CHUNKS, [1, ALL_CHUNKS])
        at, lo_hi_col = part(at, ALL_CHUNKS, [1, 2])
        at, lo_hi_row = part(at, 1, [2, ALL_CHUNKS])
        at, windows_i = part(at, 1, [2, ALL_CHUNKS], I32)
        at, windows_f = part(at, 1, [2, ALL_CHUNKS])
        at, g_dst = part(at, GROUPS, [GT, P], I32)
        at, g_lo_hi = part(at, GROUPS, [2, GT])
        at, g_wide = part(at, GROUPS, [2, GT])
        at, g_bad = part(at, GROUPS, [1, 8])
        at, slot_far = part(at, NS, [2, GT])
        at, g_row = part(at, 1, [1, GROUPS])
        at, g_worst = part(at, 1, [1, 2])
        at, calm = part(at, 1, [4, LATE_CHUNKS])
        assert at <= HI * NS
        w_both = sb("w_both", [F, 2 * F])
        w_t = sb("w_t", [2 * F, 2 * F])
        w_mean = sb("w_mean", [2 * F, 1])
        x_total = sb("x_total", [P, HI])
        size = 2 * J * F
        square = room[:, 0:size].rearrange("p (b j f) -> p b j f", b=2, j=J)
        var, std, rstd = (room[:, size + n * HI:size + (n + 1) * HI] for n in range(3))

        window_ps = ps("window_ps", [P, 512])
        count_ps = [ps(f"count_ps{b}", [P, 2, 512]) for b in range(2)]
        x_sums_ps = ps("x_sums_ps", [P, 512])
        attr_ps = ps("attr_ps", [P, 512])
        turn_ps = ps("turn_ps", [P, 512])
        table_ps, row_ps, w_t_ps = count_ps[0][:, 0, :], count_ps[0][:, 1, :], count_ps[1][:, 1, :]
        out_ps = [count_ps[b][:, :, :].rearrange("p a (j f) -> p (a j) f", f=2 * F) for b in range(2)]
        slot_rows_ps = x_sums_ps[0:NS, P:P + 2 * F]
        slot_window_ps = turn_ps[:, 256:256 + WIN]
        REL_COL = (W0 + 1) * GT

        dst_loaded = sem("dst_loaded")
        g_dst_loaded = sem("g_dst_loaded")
        w_loaded = sem("w_loaded")
        x_tab_loaded = sem("x_tab_loaded")
        pool_made = sem("pool_made")
        consts_ready = sem("consts_ready")
        dve_step = sem("dve_step")
        col_ready = sem("col_ready")
        rows_turned = sem("rows_turned")
        tables_ready = sem("tables_ready")
        w_turned = sem("w_turned")
        w_t_ready = sem("w_t_ready")
        src_landed = [sem(f"src_landed{s}") for s in range(SLOTS)]
        edge_landed = [sem(f"edge_landed{s}") for s in range(SLOTS)]
        gathers_begun = sem("gathers_begun")
        gathered = [[sem(f"gathered{s}_{q}") for q in range(PARTS)] for s in range(SLOTS)]
        slot_free = [sem(f"slot_free{s}") for s in range(SLOTS)]
        scatter_ready = [sem(f"scatter_ready{q}") for q in range(PARTS)]
        part_used = [sem(f"part_used{q}") for q in range(PARTS - PART_BUFS)]
        window_summed = sem("window_summed")
        window_added = sem("window_added")
        left_ready = sem("left_ready")
        g_rows_landed = sem("g_rows_landed")
        g_attr_landed = sem("g_attr_landed")
        prepared = sem("prepared")
        prep_step = sem("prep_step")
        turned = sem("turned")
        cols_ready = sem("cols_ready")
        hot_rel_ready = sem("hot_rel_ready")
        hot_ready = sem("hot_ready")
        counted = sem("counted")
        counts_read = sem("counts_read")
        attr_read = sem("attr_read")
        x_summed = sem("x_summed")
        x_read = sem("x_read")
        slots_turned = sem("slots_turned")
        slots_read = sem("slots_read")
        slots_hot = sem("slots_hot")
        slots_multiplied = sem("slots_multiplied")
        slots_added = sem("slots_added")
        sums_ready = sem("sums_ready")
        out_multiplied = sem("out_multiplied")
        out_added = sem("out_added")
        totals_ready = sem("totals_ready")
        centred = sem("centred")
        squared = sem("squared")
        var_ready = sem("var_ready")
        std_ready = sem("std_ready")
        rstd_ready = sem("rstd_ready")
        act_scaled = sem("act_scaled")
        pool_scaled = sem("pool_scaled")
        stored = sem("stored")

        block = ctx.enter_context(nc.Block())

        def by_partition(dram, c):
            return dram[bass.ds(c * CHUNK, CHUNK)].rearrange("(p k) -> p k", k=TILES)

        def tiles_of(g):
            return GT0 if isinstance(g, int) and g == 0 else GT

        def edges_of(g):
            if isinstance(g, int) and g == 0:
                return bass.ds(COUNTED_FROM, GT0 * P)
            return bass.ds(COUNTED_FROM + GT0 * P + (g - 1) * GROUP, GROUP)

        def tiles_before(g):
            return 0 if isinstance(g, int) and g == 0 else (g - 1) * GT + GT0

        weights = weight.rearrange("e a -> (e a)")

        def is_narrow(eng):
            return eng.value_load(flag_tab[0:1, 0:1], min_val=0, max_val=1)

        def is_calm(eng):
            return eng.value_load(flag_tab[0:1, 1:2], min_val=0, max_val=1)

        def at_slot(c):
            return c, c % SLOTS, c // SLOTS

        def round_steps(r):
            i = 0
            for n, size in enumerate(STEPS):
                chunks = [(r * ROUND_CHUNKS + k, k % SLOTS, r * (ROUND_CHUNKS // SLOTS) + k // SLOTS)
                          for k in range(i, i + size)]
                yield r * ROUND_GROUPS + n + 1, chunks
                i += size

        def each_chunk(eng, first, until, do):
            rounds = range(-(-first // SLOTS), until // SLOTS)
            for c in range(first, rounds[0] * SLOTS):
                do(*at_slot(c))
            with eng.Fori(rounds[0], rounds[-1] + 1) as r:
                for s in range(SLOTS):
                    do(r * SLOTS + s, s, r)
            for c in range((rounds[-1] + 1) * SLOTS, until):
                do(*at_slot(c))

        @block.sync
        def _(sp):
            def load_src(c, s):
                sp.dma_start(src_sb[s][:, :], by_partition(src, c)).then_inc(src_landed[s], 16)

            def load_rest(c, s):
                sp.dma_start(dst_sb[s][:, :], by_partition(dst, c)).then_inc(edge_landed[s], 16)
                sp.dma_start(w_sb[s][:, :], by_partition(weights, c)).then_inc(edge_landed[s], 16)
                sp.dma_start(rows[:, s, :, F:2 * F],
                             attr[bass.ds(c * CHUNK, CHUNK), :].rearrange("(p k) f -> p k f", k=TILES)
                             ).then_inc(edge_landed[s], 16)

            def load_chunk(c, s, r):
                sp.wait_ge(slot_free[s], r + 1)
                load_src(c, s)
                load_rest(c, s)

            for s in range(SLOTS):
                load_src(s, s)
            sp.dma_start(dst_i[:, 0, :], dst.rearrange("(c e) -> c e", e=CHUNK)).then_inc(dst_loaded, 16)
            sp.dma_start(g_dst[1:GROUPS, :, :], dst[COUNTED_FROM + GT0 * P:EDGES].rearrange(
                "(g t e) -> g t e", t=GT, e=P)).then_inc(g_dst_loaded, 16)
            for t0 in range(0, GT, GT0):
                n = min(GT0, GT - t0)
                sp.dma_start(g_dst[0:1, t0:t0 + n, :], dst[COUNTED_FROM:COUNTED_FROM + n * P].rearrange(
                    "(a t e) -> a t e", a=1, e=P)).then_inc(g_dst_loaded, 16)
            sp.dma_start(w_both[:, 0:F], node_w).then_inc(w_loaded, 16)
            sp.dma_start(w_both[:, F:2 * F], review_w).then_inc(w_loaded, 16)
            for s in range(SLOTS):
                load_rest(s, s)
            each_chunk(sp, SLOTS, CHUNKS, load_chunk)
            sp.wait_ge(tables_ready, 1)
            with sp.If(is_narrow(sp) == 0):
                each_chunk(sp, CHUNKS, ALL_CHUNKS, load_chunk)
            for n, b in enumerate(early + late):
                h0, j = blocks[b]
                if n < ACT_BLOCKS:
                    sp.wait_ge(act_scaled, n + 1)
                else:
                    sp.wait_ge(pool_scaled, n - ACT_BLOCKS + 1)
                whole = min(j, BY_P - h0)
                sp.dma_start(out[h0 * P:(h0 + whole) * P, :].rearrange("(h l) f -> l h f", l=P),
                             x_tab[:, h0:h0 + whole, :]).then_inc(stored, 16)
                if whole < j:
                    sp.dma_start(out[BY_P * P:NODES, :], x_tab[0:NODES - BY_P * P, BY_P, :]).then_inc(stored, 16)
            sp.wait_ge(stored, 16 * (BLOCKS + (BY_P < HI)))

        @block.gpsimd
        def _(pool):
            def gather_chunk(c, s, r):
                pool.wait_ge(src_landed[s], (r + 1) * 16)
                pool.wait_ge(slot_free[s], r + 1)
                pool.sem_inc(gathers_begun, 1)
                for k in range(TILES):
                    pool.indirect_dma_start(
                        out=rows[:, s, k, 0:F], out_offset=None, in_=x,
                        in_offset=bass.IndirectOffsetOnAxis(ap=src_sb[s][:, k:k + 1].bitcast(U32), axis=0),
                    ).then_inc(gathered[s][k // PER_PART], 16)

            pool.memset(ident[:, :], 0.0).then_inc(pool_made, 1)
            pool.memset(spread[:, :], 1.0).then_inc(pool_made, 1)
            pool.memset(fold[:, :], 0.0).then_inc(pool_made, 1)
            pool.iota(count16[:, :], pattern=[[1, HI * SPAN]], base=0, channel_multiplier=0,
                      allow_small_or_imprecise_dtypes=True).then_inc(pool_made, 1)
            pool.iota(column[:, :], pattern=[[1, WIN]], base=0, channel_multiplier=0,
                      allow_small_or_imprecise_dtypes=True).then_inc(pool_made, 1)
            pool.iota(slot_far[:, 0, :], pattern=[[-SPAN, GT]], base=0, channel_multiplier=1,
                      allow_small_or_imprecise_dtypes=True).then_inc(pool_made, 1)
            pool.wait_ge(pool_made, 6)
            pool.affine_select(out=ident[:, :], in_=ident[:, :], compare_op=ALU.not_equal, fill=1.0,
                               base=0, pattern=[[-1, P]], channel_multiplier=1).then_inc(pool_made, 1)
            pool.affine_select(out=fold[:, :], in_=fold[:, :], compare_op=ALU.not_equal, fill=1.0,
                               base=0, pattern=[[-1, F]], channel_multiplier=1).then_inc(pool_made, 1)
            pool.affine_select(out=spread[:, :], in_=spread[:, :], compare_op=ALU.is_ge, fill=0.0,
                               base=0, pattern=[[1, NS]], channel_multiplier=-SPAN).then_inc(pool_made, 1)
            pool.wait_ge(pool_made, 9)
            pool.affine_select(out=fold[:, :], in_=fold[:, :], compare_op=ALU.not_equal, fill=1.0,
                               base=-F, pattern=[[-1, F]], channel_multiplier=1).then_inc(pool_made, 1)
            pool.affine_select(out=spread[:, :], in_=spread[:, :], compare_op=ALU.is_ge, fill=0.0,
                               base=SPAN - 1, pattern=[[-1, NS]], channel_multiplier=SPAN).then_inc(pool_made, 1)

            each_chunk(pool, 0, CHUNKS, gather_chunk)
            pool.wait_ge(tables_ready, 1)
            with pool.If(is_narrow(pool) == 0):
                each_chunk(pool, CHUNKS, ALL_CHUNKS, gather_chunk)
            for n, b in enumerate((early + late)[ACT_BLOCKS:]):
                h0, j = blocks[b]
                y = x_tab[:, h0:h0 + j, :]
                pool.wait_ge(rstd_ready, ACT_BLOCKS + n + 1)
                pool.tensor_tensor(y, y, rstd[:, h0:h0 + j].unsqueeze(2).to_broadcast([P, j, F]), ALU.mult
                                   ).then_inc(pool_scaled, 1)

        @block.vector
        def _(dve):
            steps = 0

            def step(ins):
                nonlocal steps
                steps += 1
                ins.then_inc(dve_step, 1)
                dve.wait_ge(dve_step, steps)

            def add_chunk(c, s, r, first=None):
                base = dve.value_load(base_tab[0:1, bass.ds(c, 1)], min_val=0, max_val=NODES - 1)
                if first is None:
                    first = dve.value_load(window_tab[0:1, bass.ds(c, 1)], min_val=0, max_val=ALL_WINDOWS)
                until = dve.value_load(window_tab[0:1, bass.ds(c + 1, 1)], min_val=0, max_val=ALL_WINDOWS)
                dve.wait_ge(edge_landed[s], (r + 1) * 48)
                dve.wait_ge(left_ready, first + c + 1)
                dve.tensor_scalar(dst_left[:, :], dst_sb[s][:, :], lo_all[:, bass.ds(c, 1)], None, ALU.subtract
                                  ).then_inc(left_ready, 1)
                with dve.Fori(first, until) as w:
                    dve.wait_ge(left_ready, w + c + 2)
                    for q in range(PARTS):
                        if q >= PART_BUFS:
                            dve.wait_ge(part_used[q - PART_BUFS], w + 1)
                        for i in range(PER_PART):
                            k = q * PER_PART + i
                            made = dve.tensor_scalar(scatter[:, q % PART_BUFS, i, :], column[:, :],
                                                     dst_left[:, k:k + 1], w_sb[s][:, k:k + 1],
                                                     ALU.is_equal, ALU.mult)
                        made.then_inc(scatter_ready[q], 1)
                    dve.wait_ge(window_summed, w + 1)
                    dve.wait_ge(window_added, w + 1)
                    dve.tensor_scalar(dst_left[:, :], dst_left[:, :], float(WIN), None, ALU.subtract
                                      ).then_inc(left_ready, 1)
                    to = nc.s_assert_within(
                        base + (w - first) * WIN, 0, NODES - 1, skip_runtime_bounds_check_because=
                        "a chunk's last window begins at or before its largest dst, which is a node")
                    dve.tensor_tensor(sums[:, bass.ds(to, WIN)], sums[:, bass.ds(to, WIN)],
                                      window_ps[:, 0:WIN], ALU.add).then_inc(window_added, 1)
                dve.sem_inc(slot_free[s], 1)
                return until

            def prepare(g):
                nt = tiles_of(g)
                dve.wait_ge(g_rows_landed, (g + 1) * 48)
                if not (isinstance(g, int) and g == 0):
                    dve.wait_ge(turned, g)
                src_i, dst_i, w_i = g_idx[0:nt, 0, :], g_idx[0:nt, 1, :], g_w[0:nt, :]
                cut, pack, parts = w_cut[0:nt, :, :], packed[0:nt, :, :], hi_lo[0:nt, :, :]
                dve.tensor_reduce(tile_first[0:nt, :], dst_i, AX_X, ALU.min).then_inc(prep_step, 1)
                dve.tensor_scalar(parts[:, 0, :], src_i, LO_BITS, None, ALU.arith_shift_right)
                dve.tensor_scalar(parts[:, 1, :], src_i, P - 1, None, ALU.bitwise_and)
                dve.tensor_copy(cut[:, 0, :], w_i).then_inc(prep_step, 1)
                dve.wait_ge(prep_step, 5 * g + 2)
                dve.tensor_scalar(pack[:, REL, :], dst_i, tile_first[0:nt, 0:1], None, ALU.subtract)
                dve.tensor_tensor(pack[:, W1, :], w_i, cut[:, 0, :], ALU.subtract).then_inc(prep_step, 1)
                dve.wait_ge(prep_step, 5 * g + 3)
                dve.tensor_copy(cut[:, 1, :], pack[:, W1, :]).then_inc(prep_step, 1)
                dve.scalar_tensor_tensor(pack[:, KEY, :], parts[:, 0, :], float(SPAN), pack[:, REL, :],
                                         ALU.mult, ALU.add)
                dve.tensor_copy(pack[:, LO, :], parts[:, 1, :]).then_inc(prep_step, 1)
                dve.wait_ge(prep_step, 5 * g + 5)
                dve.tensor_tensor(pack[:, W2, :], pack[:, W1, :], cut[:, 1, :], ALU.subtract
                                  ).then_inc(prepared, 1)

            def make_hot(g, tiles):
                n0 = tiles_before(g)
                for t in tiles:
                    h = t % HOT_BUFS
                    if t >= HOT_BUFS:
                        dve.wait_ge(counted, n0 + t - HOT_BUFS + 1)
                    dve.tensor_scalar(hot_key[h][:, :], count16[:, :], cols[:, KEY, t:t + 1], None, ALU.is_equal)
                    for i, part in enumerate((W0, W1, W2)):
                        made = dve.tensor_scalar(hot_lo[h][:, i, :], count16[:, 0:P], cols[:, LO, t:t + 1],
                                                 cols[:, part, t:t + 1], ALU.is_equal, ALU.mult)
                    made.then_inc(hot_ready, 1)

            def begin_hot(g):
                dve.wait_ge(cols_ready, g + 1)
                n0, nt = tiles_before(g), tiles_of(g)
                if not (isinstance(g, int) and g == 0):
                    dve.wait_ge(counted, n0)
                rel = hot_rel[:, 0:nt, :]
                dve.tensor_tensor(rel, column[:, 0:SPAN].unsqueeze(1).to_broadcast([P, nt, SPAN]),
                                  cols[:, REL, 0:nt].unsqueeze(2).to_broadcast([P, nt, SPAN]), ALU.is_equal
                                  ).then_inc(hot_rel_ready, 1)
                dve.wait_ge(hot_rel_ready, g * 2 + 1)
                dve.tensor_tensor(rel, rel, cols[:, W0, 0:nt].unsqueeze(2).to_broadcast([P, nt, SPAN]), ALU.mult
                                  ).then_inc(hot_rel_ready, 1)
                make_hot(g, range(HOT_BUFS))

            def make_slots_hot(g):
                dve.wait_ge(cols_ready, g + 1)
                dve.tensor_scalar(slot_scatter[:, :], column[0:NS, :], slot_rel[:, 0:1], None, ALU.is_equal
                                  ).then_inc(slots_hot, 1)

            def add_slots(g, until):
                base = dve.value_load(group_tab[0:1, bass.ds(g, 1)], min_val=0, max_val=NODES - 1)
                dve.wait_ge(window_added, until + 1)
                dve.wait_ge(slots_multiplied, g + 1)
                dve.tensor_tensor(sums[:, bass.ds(base, WIN)], sums[:, bass.ds(base, WIN)],
                                  slot_window_ps, ALU.add).then_inc(slots_added, 1)
                dve.wait_ge(slots_added, g + 1)

            def total_nodes():
                dve.wait_ge(x_tab_loaded, 32 if NODES % P else 16)
                for h0, j in blocks:
                    made = dve.tensor_reduce(x_total[:, h0:h0 + j], x_tab[:, h0:h0 + j, :], AX_X, ALU.add)
                made.then_inc(totals_ready, 1)
                dve.wait_ge(totals_ready, 1)

            def centre(b):
                h0, j = blocks[b]
                y = x_tab[:, h0:h0 + j, :]
                dve.scalar_tensor_tensor(y, x_total[:, h0:h0 + j].unsqueeze(2).to_broadcast([P, j, F]), -1.0 / F, y,
                                         ALU.mult, ALU.add).then_inc(centred, 1)

            def finish(which, before):
                centre(which[0])
                for n in range(len(which) + 2):
                    if n < len(which):
                        h0, j = blocks[which[n]]
                        y = x_tab[:, h0:h0 + j, :]
                        dve.wait_ge(centred, before + n + 1)
                        dve.wait_ge(out_multiplied, before + n + 1)
                        dve.tensor_tensor(y, y, out_ps[(before + n) % 2][:, 0:j, 0:F], ALU.add).then_inc(out_added, 1)
                    if n + 1 < len(which):
                        centre(which[n + 1])
                    if 1 <= n <= len(which):
                        h0, j = blocks[which[n - 1]]
                        dve.wait_ge(squared, before + n)
                        dve.tensor_reduce(var[:, h0:h0 + j], square[:, (before + n - 1) % 2, 0:j, :], AX_X, ALU.add
                                          ).then_inc(var_ready, 1)
                    if n >= 2:
                        h0, j = blocks[which[n - 2]]
                        dve.wait_ge(std_ready, before + n - 1)
                        dve.reciprocal(rstd[:, h0:h0 + j], std[:, h0:h0 + j]).then_inc(rstd_ready, 1)

            def sums_are_ready(until):
                dve.wait_ge(window_added, until + 1)
                dve.sem_inc(sums_ready, 1)

            for s in range(SLOTS):
                dve.sem_inc(slot_free[s], 1)
            dve.memset(ones, 1.0)
            dve.memset(eps[:, :], LN_EPS)
            dve.memset(x_sums[:, :], 0.0)
            dve.memset(attr_sums[:, :], 0.0)
            dve.memset(slot_rel[:, :], -1.0)
            dve.memset(x_tab[:, HI - 1, :], 0.0).then_inc(consts_ready, 1)
            dve.memset(sums[:, :], 0.0).then_inc(window_added, 1)
            dve.wait_ge(pool_made, 11)
            step(dve.tensor_scalar(slot_far[:, 1, :], slot_far[:, 0, :], 0.0, float(P), ALU.is_lt, ALU.mult))
            step(dve.scalar_tensor_tensor(slot_far[:, 1, :], slot_far[:, 1, :], float(P), slot_far[:, 0, :],
                                          ALU.mult, ALU.add))
            dve.tensor_reduce(slot_no[:, :], slot_far[:, 1, :], AX_X, ALU.min)
            dve.tensor_scalar(spread[0:1, :], spread[0:1, :], 1.0, None, ALU.subtract)
            dve.wait_ge(dst_loaded, 16)
            dve.tensor_reduce(lo_hi_col[:, 0, 1:2], dst_i[:, 0, :], AX_X, ALU.max)
            step(dve.tensor_reduce(lo_hi_col[:, 0, 0:1], dst_i[:, 0, :], AX_X, ALU.min))
            dve.tensor_scalar(lo_diag[:, 0, :], ident[0:ALL_CHUNKS, 0:ALL_CHUNKS], lo_hi_col[:, 0, 0:1], None, ALU.mult)
            dve.wait_ge(g_dst_loaded, G_DST_DMAS * 16)
            dve.tensor_reduce(g_lo_hi[:, 0, :], g_dst, AX_X, ALU.min)
            step(dve.tensor_reduce(g_lo_hi[:, 1, :], g_dst, AX_X, ALU.max))
            dve.tensor_tensor(g_wide[:, 0, :], g_lo_hi[:, 1, :], g_lo_hi[:, 0, :], ALU.subtract)
            step(dve.tensor_scalar(g_wide[:, 1, :], g_lo_hi[:, 0, :], g_lo_hi[:, 0, 0:1], None, ALU.subtract))
            dve.tensor_reduce(g_bad[:, 0, 0:1], g_wide[:, 0, :], AX_X, ALU.max)
            dve.tensor_reduce(g_bad[:, 0, 1:2], g_wide[:, 1, :], AX_X, ALU.max)
            step(dve.tensor_reduce(g_bad[:, 0, 2:3], g_wide[:, 1, :], AX_X, ALU.min))
            dve.tensor_scalar(g_bad[:, 0, 3:4], g_bad[:, 0, 0:1], float(SPAN), None, ALU.is_ge)
            dve.tensor_scalar(g_bad[:, 0, 4:5], g_bad[:, 0, 1:2], float(WIN - SPAN + 1), None, ALU.is_ge)
            step(dve.tensor_scalar(g_bad[:, 0, 5:6], g_bad[:, 0, 2:3], 0.0, None, ALU.is_lt))
            step(dve.tensor_tensor(g_bad[:, 0, 6:7], g_bad[:, 0, 3:4], g_bad[:, 0, 4:5], ALU.add))
            dve.tensor_tensor(g_bad[:, 0, 7:8], g_bad[:, 0, 6:7], g_bad[:, 0, 5:6], ALU.add).then_inc(col_ready, 1)
            dve.wait_ge(rows_turned, 1)
            dve.tensor_copy(lo_hi_row, row_ps[0:1, 0:2 * ALL_CHUNKS].rearrange("p (a c) -> p a c", a=2))
            dve.tensor_copy(g_row[:, 0, :], row_ps[0:1, 256:256 + GROUPS])
            dve.tensor_copy(group_tab[:, :], row_ps[0:1, 320:320 + GROUPS])
            step(dve.tensor_copy(lo_all[:, :], table_ps[:, 0:ALL_CHUNKS]))
            dve.tensor_copy(base_tab[0:1, :], lo_hi_row[:, 0, :])
            step(dve.tensor_tensor(windows_i[:, 0, :], lo_hi_row[:, 1, :], lo_hi_row[:, 0, :], ALU.subtract))
            step(dve.tensor_scalar(windows_i[:, 1, :], windows_i[:, 0, :], WIN_SHIFT, None, ALU.arith_shift_right))
            step(dve.tensor_scalar(windows_f[:, 0, :], windows_i[:, 1, :], 1.0, None, ALU.add))
            step(dve.tensor_tensor_scan(windows_f[:, 1, :], ones[0:1, 0, 0:ALL_CHUNKS], windows_f[:, 0, :], 0.0,
                                        ALU.mult, ALU.add))
            dve.memset(window_tab[:, 0:1], 0)
            dve.tensor_copy(window_tab[:, 1:ALL_CHUNKS + 1], windows_f[:, 1, :])
            dst_of_late = lo_hi_row[:, :, CHUNKS - LATE_CHUNKS:CHUNKS]
            dve.tensor_scalar(calm[:, 0, :], dst_of_late[:, 0, :], float(LATE_NODES[0]), None, ALU.is_ge)
            step(dve.tensor_scalar(calm[:, 1, :], dst_of_late[:, 1, :], float(LATE_NODES[1] - WIN), None, ALU.is_lt))
            step(dve.tensor_tensor(calm[:, 2, :], calm[:, 0, :], calm[:, 1, :], ALU.mult))
            step(dve.tensor_reduce(calm[:, 3, 0:1], calm[:, 2, :], AX_X, ALU.min))
            dve.tensor_copy(flag_tab[:, 1:2], calm[:, 3, 0:1])
            step(dve.tensor_reduce(g_worst[:, 0, 0:1], g_row[:, 0, :], AX_X, ALU.max))
            dve.tensor_scalar(flag_tab[:, 0:1], g_worst[:, 0, 0:1], 0.0, None, ALU.is_equal).then_inc(tables_ready, 1)
            dve.wait_ge(w_turned, 1)
            step(dve.tensor_reduce(w_mean[:, :], w_t_ps[:, 0:F], AX_X, ALU.add))
            step(dve.tensor_scalar(w_mean[:, :], w_mean[:, :], 1.0 / F, None, ALU.mult))
            for a in range(2):
                made = dve.tensor_scalar(w_t[:, a * F:(a + 1) * F], w_t_ps[:, 0:F], w_mean[:, 0:1], None, ALU.subtract)
            made.then_inc(w_t_ready, 1)
            dve.wait_ge(tables_ready, 1)
            dve.sem_inc(left_ready, 1)
            narrow = is_narrow(dve)
            dve.wait_ge(g_rows_landed, 48)
            with dve.If(narrow == 1):
                prepare(0)
                begin_hot(0)
                make_hot(0, range(HOT_BUFS, GT0))
                make_slots_hot(0)
                prepare(1)
                begin_hot(1)

                def step_of(g, chunks):
                    until = add_chunk(*chunks[0])
                    make_hot(g, range(HOT_BUFS, GT))
                    for chunk in chunks[1:]:
                        until = add_chunk(*chunk, until)
                    add_slots(g - 1, until)
                    make_slots_hot(g)
                    if not (isinstance(g, int) and g == GROUPS - 1):
                        prepare(g + 1)
                        begin_hot(g + 1)
                    return until

                with dve.Fori(0, ROUNDS) as r:
                    for g, chunks in round_steps(r):
                        step_of(g, chunks)
                for g, chunks in last_steps:
                    until = step_of(g, [at_slot(c) for c in chunks])
                total_nodes()
                for c in last_chunks:
                    until = add_chunk(*at_slot(c), until)
                add_slots(GROUPS - 1, until)
                dve.wait_ge(x_summed, GROUPS)
                calm_now = is_calm(dve)
                with dve.If(calm_now == 1):
                    sums_are_ready(until)
                    finish(early, 0)
                for c in range(CHUNKS - LATE_CHUNKS, CHUNKS):
                    until = add_chunk(*at_slot(c), until)
                sums_are_ready(until)
                with dve.If(calm_now == 0):
                    dve.sem_inc(sums_ready, 1)
                    finish(early, 0)
            with dve.Else():
                each_chunk(dve, 0, ALL_CHUNKS - 1, add_chunk)
                total_nodes()
                sums_are_ready(add_chunk(*at_slot(ALL_CHUNKS - 1)))
                dve.sem_inc(sums_ready, 1)
                finish(early, 0)
            finish(late, len(early))

        @block.scalar
        def _(act):
            def load_rows(g):
                nt = tiles_of(g)
                for dram, to in ((src, g_idx[0:nt, 0, :]), (dst, g_idx[0:nt, 1, :]), (weights, g_w[0:nt, :])):
                    act.dma_start(to, dram[edges_of(g)].rearrange("(t e) -> t e", e=P)).then_inc(g_rows_landed, 16)

            def load_attr(g):
                act.dma_start(g_attr[:, 0:tiles_of(g), :], attr[edges_of(g), :].rearrange("(t e) f -> e t f", e=P)
                              ).then_inc(g_attr_landed, 16)

            def read_cols(g):
                act.wait_ge(turned, g + 1)
                if not isinstance(g, int) or g >= 1:
                    act.wait_ge(slots_hot, g)
                nt = tiles_of(g)
                act.activation(slot_rel[0:nt * SPAN, :], turn_ps[0:nt * SPAN, REL_COL:REL_COL + 1], ACT.Identity,
                               bias=slot_no[0:nt * SPAN, 0:1])
                act.activation(cols[:, :, 0:nt], turn_ps[:, 0:REL_COL].rearrange("p (q t) -> p q t", t=GT)[:, :, 0:nt],
                               ACT.Copy).then_inc(cols_ready, 1)

            def read_slots(g):
                act.wait_ge(slots_turned, g + 1)
                act.activation(slot_rows[:, :], slot_rows_ps, ACT.Copy).then_inc(slots_read, 1)

            def read_counts(g):
                n0, ns = tiles_before(g), tiles_of(g) * SPAN
                for t in range(tiles_of(g)):
                    act.wait_ge(counted, n0 + t + 1)
                    if t == 0 and not (isinstance(g, int) and g == 0):
                        act.wait_ge(x_summed, g)
                    act.activation(
                        counts[:, :, t * SPAN:(t + 1) * SPAN].rearrange("p (a h) d -> p a h d", a=2),
                        count_ps[t % 2][:, :, 0:HALF].rearrange("p a (h d) -> p a h d", d=SPAN), ACT.Copy
                    ).then_inc(counts_read, 1)
                for odd in range(2):
                    half = slice(odd * F, (odd + 1) * F)
                    tiles = slice(odd, tiles_of(g), 2)
                    last = act.activation(attr_sums[half, :].rearrange("p (t d) -> p t d", d=SPAN)[:, tiles, :],
                                          attr_ps[half, 0:NS].rearrange("p (t d) -> p t d", d=SPAN)[:, tiles, :],
                                          ACT.Copy)
                last.then_inc(attr_read, 1)

            def read_x_sums(g):
                act.wait_ge(x_summed, g + 1)
                ns = tiles_of(g) * SPAN
                act.activation(x_sums[:, 0:ns], x_sums_ps[:, 0:ns], ACT.Copy).then_inc(x_read, 1)

            load_rows(0)
            load_attr(0)
            act.wait_ge(consts_ready, 1)
            act.wait_ge(dst_loaded, 16)
            act.wait_ge(g_dst_loaded, G_DST_DMAS * 16)
            act.dma_start(x_tab[:, 0:BY_P, :], x[0:BY_P * P, :].rearrange("(h l) f -> l h f", l=P)
                          ).then_inc(x_tab_loaded, 16)
            if BY_P < HI:
                act.dma_start(x_tab[0:NODES - BY_P * P, BY_P, :], x[BY_P * P:NODES, :]).then_inc(x_tab_loaded, 16)
            act.wait_ge(tables_ready, 1)
            with act.If(is_narrow(act) == 1):
                read_cols(0)
                load_rows(1)
                read_counts(0)
                load_attr(1)
                read_cols(1)
                load_rows(2)
                read_x_sums(0)

                def step_of(g):
                    read_slots(g - 1)
                    read_counts(g)
                    if not (isinstance(g, int) and g == GROUPS - 1):
                        load_attr(g + 1)
                        read_cols(g + 1)
                        if not (isinstance(g, int) and g == GROUPS - 2):
                            load_rows(g + 2)
                    read_x_sums(g)

                with act.Fori(0, ROUNDS) as r:
                    for g, _ in round_steps(r):
                        step_of(g)
                for g, _ in last_steps:
                    step_of(g)
                read_slots(GROUPS - 1)
            def square_and_root(n):
                h0, j = blocks[(early + late)[n]]
                act.wait_ge(out_added, n + 1)
                if n >= 2:
                    act.wait_ge(var_ready, n - 1)
                act.activation(square[:, n % 2, 0:j, :], x_tab[:, h0:h0 + j, :], ACT.Square).then_inc(squared, 1)
                act.wait_ge(var_ready, n + 1)
                act.activation(std[:, h0:h0 + j], var[:, h0:h0 + j], ACT.Sqrt, bias=eps[:, :], scale=1.0 / F
                               ).then_inc(std_ready, 1)

            for n in range(len(early)):
                square_and_root(n)
            for n in range(ACT_BLOCKS):
                h0, j = blocks[early[n]]
                act.wait_ge(rstd_ready, n + 1)
                for h in range(h0, h0 + j):
                    last = act.activation(x_tab[:, h, :], x_tab[:, h, :], ACT.Copy, scale=rstd[:, h:h + 1])
                last.then_inc(act_scaled, 1)
            for n in range(len(early), BLOCKS):
                square_and_root(n)

        @block.tensor
        def _(pe):
            def sum_chunk(c, s, r, first=None):
                if first is None:
                    first = pe.value_load(window_tab[0:1, bass.ds(c, 1)], min_val=0, max_val=ALL_WINDOWS)
                until = pe.value_load(window_tab[0:1, bass.ds(c + 1, 1)], min_val=0, max_val=ALL_WINDOWS)
                with pe.Fori(first, until) as w:
                    pe.wait_ge(edge_landed[s], (r + 1) * 48)
                    pe.wait_ge(window_added, w + 1)
                    for k in range(TILES):
                        if k % PER_PART == 0:
                            pe.wait_ge(scatter_ready[k // PER_PART], w + 1)
                            pe.wait_ge(gathered[s][k // PER_PART], (r + 1) * (16 * PER_PART))
                        q, i = divmod(k, PER_PART)
                        done = pe.matmul(window_ps[:, 0:WIN], rows[:, s, k, :], scatter[:, q % PART_BUFS, i, :],
                                         start=(k == 0), stop=(k == TILES - 1))
                        if i == PER_PART - 1 and q < PARTS - PART_BUFS:
                            done.then_inc(part_used[q], 1)
                    done.then_inc(window_summed, 1)
                return until

            def turn_cols(g):
                pe.wait_ge(prepared, g + 1)
                if not isinstance(g, int) or g >= 2:
                    pe.wait_ge(slots_added, g - 1)
                if not isinstance(g, int) or g >= 1:
                    pe.wait_ge(cols_ready, g)
                nt = tiles_of(g)
                pe.matmul(turn_ps[0:nt * SPAN, REL_COL:REL_COL + 1], spread[0:nt, 0:nt * SPAN], tile_first[0:nt, 0:1],
                          start=True, stop=True)
                for q in range(W0):
                    pe.transpose(turn_ps[:, q * GT:q * GT + nt], packed[0:nt, q, :], ident[0:nt, 0:nt])
                pe.transpose(turn_ps[:, W0 * GT:W0 * GT + nt], g_w[0:nt, :], ident[0:nt, 0:nt]).then_inc(turned, 1)

            def count_tiles(g):
                pe.wait_ge(g_attr_landed, (g + 1) * 16)
                if not isinstance(g, int) or g >= 1:
                    pe.wait_ge(attr_read, g)
                n0 = tiles_before(g)
                for t in range(tiles_of(g)):
                    h, b = t % HOT_BUFS, t % 2
                    pe.wait_ge(hot_ready, n0 + t + 1)
                    if t % 2 == 0:
                        until = min(t + 2, tiles_of(g))
                        pe.matmul(attr_ps[0:(until - t) * F, t * SPAN:until * SPAN],
                                  g_attr[:, t:until, :].rearrange("p t f -> p (t f)"),
                                  hot_rel[:, t:until, :].rearrange("p t d -> p (t d)"), start=True, stop=True)
                    if not (isinstance(g, int) and n0 + t < 2):
                        pe.wait_ge(counts_read, n0 + t - 1)
                    for i in range(3):
                        for a in range(2):
                            last = pe.matmul(count_ps[b][:, a, 0:HALF], hot_lo[h][:, i, :],
                                             hot_key[h][:, a * HALF:(a + 1) * HALF], start=(i == 0), stop=(i == 2))
                    last.then_inc(counted, 1)

            def sum_x(g):
                ns = tiles_of(g) * SPAN
                pe.wait_ge(counts_read, tiles_before(g) + tiles_of(g))
                if not isinstance(g, int) or g >= 1:
                    pe.wait_ge(slots_read, g)
                for hi in range(HI):
                    if hi == HI // 2 and not (isinstance(g, int) and g == GROUPS - 1):
                        turn_cols(g + 1)
                    half = hi % 2
                    done = pe.matmul(x_sums_ps[half * F:(half + 1) * F, 0:ns], x_tab[:, hi, :], counts[:, hi, 0:ns],
                                     start=(hi < 2), stop=(hi >= HI - 2))
                done.then_inc(x_summed, 1)

            def turn_slots(g):
                pe.wait_ge(x_read, g + 1)
                pe.wait_ge(attr_read, g + 1)
                pe.matmul(slot_rows_ps[:, 0:F], x_sums[:, :], fold[:, :], start=True, stop=True)
                pe.matmul(slot_rows_ps[:, F:2 * F], attr_sums[:, :], fold[:, :], start=True, stop=True
                          ).then_inc(slots_turned, 1)

            def multiply_slots(g):
                pe.wait_ge(slots_read, g + 1)
                pe.wait_ge(slots_hot, g + 1)
                pe.matmul(slot_window_ps, slot_rows[:, :], slot_scatter[:, :], start=True, stop=True
                          ).then_inc(slots_multiplied, 1)

            def multiply_out(which, before, ready):
                pe.wait_ge(sums_ready, ready)
                for n, b in enumerate(which, before):
                    h0, j = blocks[b]
                    if n >= 2:
                        pe.wait_ge(out_added, n - 1)
                    for i in range(j):
                        last = pe.matmul(out_ps[n % 2][:, i, :], sums[:, (h0 + i) * P:(h0 + i + 1) * P], w_t[:, :],
                                         start=True, stop=True)
                    last.then_inc(out_multiplied, 1)

            pe.wait_ge(pool_made, 11)
            pe.wait_ge(col_ready, 1)
            for a in range(2):
                pe.matmul(row_ps[0:1, a * ALL_CHUNKS:(a + 1) * ALL_CHUNKS], lo_hi_col[:, 0, a:a + 1],
                          ident[0:ALL_CHUNKS, 0:ALL_CHUNKS], start=True, stop=True)
            for at_, col in ((256, g_bad[:, 0, 7:8]), (320, g_lo_hi[:, 0, 0:1])):
                pe.matmul(row_ps[0:1, at_:at_ + GROUPS], col, ident[0:GROUPS, 0:GROUPS],
                          start=True, stop=True)
            pe.matmul(table_ps[:, 0:ALL_CHUNKS], ones[0:ALL_CHUNKS, 0, :], lo_diag[:, 0, :],
                      start=True, stop=True).then_inc(rows_turned, 1)
            pe.wait_ge(w_loaded, 32)
            pe.transpose(w_t_ps[:, 0:F], w_both[:, :], ident[0:F, 0:F]).then_inc(w_turned, 1)
            pe.wait_ge(w_t_ready, 1)
            pe.wait_ge(tables_ready, 1)
            with pe.If(is_narrow(pe) == 1):
                turn_cols(0)
                count_tiles(0)
                pe.wait_ge(x_tab_loaded, 32 if NODES % P else 16)
                sum_x(0)

                def step_of(g, chunks):
                    until = sum_chunk(*chunks[0])
                    turn_slots(g - 1)
                    count_tiles(g)
                    for chunk in chunks[1:]:
                        until = sum_chunk(*chunk, until)
                    multiply_slots(g - 1)
                    sum_x(g)

                with pe.Fori(0, ROUNDS) as r:
                    for g, chunks in round_steps(r):
                        step_of(g, chunks)
                for g, chunks in last_steps:
                    step_of(g, [at_slot(c) for c in chunks])
                until = None
                for c in last_chunks:
                    until = sum_chunk(*at_slot(c), until)
                turn_slots(GROUPS - 1)
                multiply_slots(GROUPS - 1)
                calm_now = is_calm(pe)
                with pe.If(calm_now == 1):
                    multiply_out(early, 0, 1)
                for c in range(CHUNKS - LATE_CHUNKS, CHUNKS):
                    until = sum_chunk(*at_slot(c), until)
                with pe.If(calm_now == 0):
                    multiply_out(early, 0, 2)
            with pe.Else():
                pe.wait_ge(x_tab_loaded, 32 if NODES % P else 16)
                pe.wait_ge(g_attr_landed, 16)
                each_chunk(pe, 0, ALL_CHUNKS, sum_chunk)
                multiply_out(early, 0, 2)
            multiply_out(late, len(early), 2)


INPUTS = ["x", "src", "dst", "edge_attr_64", "edge_weight1", "L0_gnn_node_w", "L0_gnn_review_w"]


def kernel(**inputs):
    import numpy as np
    import concourse.bacc as bacc
    from concourse.bass_utils import run_bass_kernel_spmd

    nc = bacc.Bacc("TRN2", target_bir_lowering=False, num_devices=1)
    arrays, args = {}, []
    for name in INPUTS:
        a = np.ascontiguousarray(inputs[name])
        arrays[name] = a
        args.append(nc.dram_tensor(name, a.shape, mybir.dt.from_np(a.dtype), kind="ExternalInput").ap())
    out = nc.dram_tensor("out", arrays["x"].shape, F32, kind="ExternalOutput").ap()
    build(nc, *args, out)
    result = run_bass_kernel_spmd(nc, [arrays], core_ids=[0])
    return result.results[0]["out"]
```
